# Optimizing a Trainium2 kernel written in Bass

```python
import numpy as np
import jax
import jax.numpy as jnp

def _softmax(x, axis=-1):
    return jax.nn.softmax(x, axis=axis)

def _gelu(x):
    return jax.nn.gelu(x, approximate=True)

def _silu(x):
    return jax.nn.silu(x)

def _sigmoid(x):
    return jax.nn.sigmoid(x)

def _layernorm(x, axis=-1, eps=1e-05):
    m = jnp.mean(x, axis=axis, keepdims=True)
    v = jnp.var(x, axis=axis, keepdims=True)
    return (x - m) / jnp.sqrt(v + eps)

def _scatter_add(tgt, idx, src, axis=0):
    return tgt.at[idx].add(src)

def _segment_sum(src, seg, n):
    return jax.ops.segment_sum(src, seg, n)
kernel_name = 'mk_audio_tower_d1_tok_audfeat512_r4_e2ca60'

def setup_inputs(seed: int=0):
    np.random.seed(seed)
    _w = jnp.asarray

    def _rec_inputs():
        import jax
        import jax.numpy as jnp
        _rk = jax.random.key(seed)
        x = 7.22013e-05 + 1.00017 * jax.random.normal(jax.random.fold_in(_rk, 1), (32, 750, 32), jnp.float32)
        return x
    x = _rec_inputs()

    def _L0_tok_setup():
        import jax, jax.numpy as jnp
        import numpy as np
        PATCH_LEN = 16
        PATCH_STRIDE = 8
        D_MODEL = 128
        N_FEATURES = 32
        key = jax.random.key(seed)
        k_x, k_w, k_b = jax.random.split(key, 3)
        x = jax.random.normal(k_x, (64, 1024, N_FEATURES), dtype=jnp.float32)
        in_dim = PATCH_LEN * N_FEATURES
        bound = 1.0 / np.sqrt(in_dim)
        W = jax.random.uniform(k_w, (D_MODEL, in_dim), dtype=jnp.float32, minval=-bound, maxval=bound)
        b = jax.random.uniform(k_b, (D_MODEL,), dtype=jnp.float32, minval=-bound, maxval=bound)
        return {'x': x, 'W': W, 'b': b}
    _L0_tok_all = _L0_tok_setup()
    _L0_tok_in = {k: v for k, v in _L0_tok_all.items() if k in ('W', 'b')}
    del _L0_tok_all

    def _L0_attn_setup():
        import jax, jax.numpy as jnp
        import numpy as np
        PI = np.float32(np.pi)

        def goom_log(x):
            return jax.lax.complex(jnp.log(jnp.abs(x)).astype(jnp.float32), jnp.where(x < 0, PI, np.float32(0.0)))

        def log_matmul_exp(LA, LB):
            c1 = jnp.max(LA.real, axis=-1, keepdims=True)
            c2 = jnp.max(LB.real, axis=-2, keepdims=True)
            c1 = jnp.where(jnp.isfinite(c1), c1, np.float32(0.0))
            c2 = jnp.where(jnp.isfinite(c2), c2, np.float32(0.0))
            P = jnp.matmul(jnp.exp(LA - c1), jnp.exp(LB - c2))
            return jnp.log(P) + c1 + c2
        key = jax.random.key(seed)
        ks = jax.random.split(key, 6)
        d_inp, d_out, n_hid, d_hid = (128, 128, 4, 64)
        Bsz, L = (8, 256)
        u = jax.random.normal(ks[0], (Bsz, L, d_inp), dtype=jnp.float32)
        init_states = jax.random.uniform(ks[1], (n_hid, d_hid), minval=-0.1, maxval=0.1, dtype=jnp.float32)
        Q, _ = jnp.linalg.qr(jax.random.normal(ks[2], (d_hid, d_hid), dtype=jnp.float32))
        A = np.float32(0.99) * Q
        B = jax.random.uniform(ks[3], (d_inp, n_hid * d_hid), minval=-1.0, maxval=1.0, dtype=jnp.float32) / np.float32(np.sqrt(d_inp))
        C = jax.random.uniform(ks[4], (n_hid * d_hid, d_out), minval=-1.0, maxval=1.0, dtype=jnp.float32) / np.float32(np.sqrt(n_hid * d_hid))
        D = jax.random.uniform(ks[5], (d_inp, d_out), minval=-1.0, maxval=1.0, dtype=jnp.float32) / np.float32(np.sqrt(d_inp))
        return {'u': u, 'init_states': init_states, 'A': A, 'B': B, 'C': C, 'D': D}
    _L0_attn_all = _L0_attn_setup()
    _L0_attn_in = {k: v for k, v in _L0_attn_all.items() if k in ('init_states', 'A', 'B', 'C', 'D')}
    del _L0_attn_all

    def _L0_ffn_setup():
        import jax, jax.numpy as jnp
        import numpy as np
        DIM = 128
        HID = 256
        E = 8
        K = 2
        B, S = (4, 512)
        key = jax.random.key(seed)
        ks = jax.random.split(key, 10)
        sd = DIM ** (-0.5)
        sh = HID ** (-0.5)
        return {'x': jax.random.normal(ks[0], (B, S, DIM), dtype=jnp.float32), 'gate_w': jax.random.normal(ks[1], (E, DIM), dtype=jnp.float32) * sd, 'biases': jnp.zeros((E,), dtype=jnp.float32), 'w1': jax.random.normal(ks[2], (E, DIM, HID), dtype=jnp.float32) * sd, 'w3': jax.random.normal(ks[3], (E, DIM, HID), dtype=jnp.float32) * sd, 'w2': jax.random.normal(ks[4], (E, HID, DIM), dtype=jnp.float32) * sh, 'sw1': jax.random.normal(ks[5], (DIM, HID), dtype=jnp.float32) * sd, 'sw3': jax.random.normal(ks[6], (DIM, HID), dtype=jnp.float32) * sd, 'sw2': jax.random.normal(ks[7], (HID, DIM), dtype=jnp.float32) * sh}
    _L0_ffn_all = _L0_ffn_setup()
    _L0_ffn_in = {k: v for k, v in _L0_ffn_all.items() if k in ('gate_w', 'biases', 'w1', 'w3', 'w2', 'sw1', 'sw3', 'sw2')}
    del _L0_ffn_all
    return {'x': x, 'L0_tok_W': _L0_tok_in['W'], 'L0_tok_b': _L0_tok_in['b'], 'L0_attn_init_states': _L0_attn_in['init_states'], 'L0_attn_A': _L0_attn_in['A'], 'L0_attn_B': _L0_attn_in['B'], 'L0_attn_C': _L0_attn_in['C'], 'L0_attn_D': _L0_attn_in['D'], 'L0_ffn_gate_w': _L0_ffn_in['gate_w'], 'L0_ffn_biases': _L0_ffn_in['biases'], 'L0_ffn_w1': _L0_ffn_in['w1'], 'L0_ffn_w3': _L0_ffn_in['w3'], 'L0_ffn_w2': _L0_ffn_in['w2'], 'L0_ffn_sw1': _L0_ffn_in['sw1'], 'L0_ffn_sw3': _L0_ffn_in['sw3'], 'L0_ffn_sw2': _L0_ffn_in['sw2']}

def reference(x, L0_tok_W, L0_tok_b, L0_attn_init_states, L0_attn_A, L0_attn_B, L0_attn_C, L0_attn_D, L0_ffn_gate_w, L0_ffn_biases, L0_ffn_w1, L0_ffn_w3, L0_ffn_w2, L0_ffn_sw1, L0_ffn_sw3, L0_ffn_sw2):
    import jax
    import jax.numpy as jnp

    def _L0_tok_ref(x, W, b):
        import jax, jax.numpy as jnp
        import numpy as np
        PATCH_LEN = 16
        PATCH_STRIDE = 8
        D_MODEL = 128
        N_FEATURES = 32
        B, T, C = x.shape
        n_patches = (T - PATCH_LEN) // PATCH_STRIDE + 1
        idx = jnp.arange(n_patches)[:, None] * PATCH_STRIDE + jnp.arange(PATCH_LEN)[None, :]
        patches = x[:, idx, :]
        patches = patches.reshape(B, n_patches, PATCH_LEN * C)
        return jnp.einsum('bpf,df->bpd', patches, W) + b

    def _L0_attn_ref(u, init_states, A, B, C, D):
        import jax, jax.numpy as jnp
        import numpy as np
        PI = np.float32(np.pi)

        def goom_log(x):
            return jax.lax.complex(jnp.log(jnp.abs(x)).astype(jnp.float32), jnp.where(x < 0, PI, np.float32(0.0)))

        def log_matmul_exp(LA, LB):
            c1 = jnp.max(LA.real, axis=-1, keepdims=True)
            c2 = jnp.max(LB.real, axis=-2, keepdims=True)
            c1 = jnp.where(jnp.isfinite(c1), c1, np.float32(0.0))
            c2 = jnp.where(jnp.isfinite(c2), c2, np.float32(0.0))
            P = jnp.matmul(jnp.exp(LA - c1), jnp.exp(LB - c2))
            return jnp.log(P) + c1 + c2
        Bsz, L, d_inp = u.shape
        n, d = init_states.shape
        Bu = jnp.matmul(u, B).reshape(Bsz, L, n, d)
        A_b = jnp.broadcast_to(A, (Bsz, L, d, d))
        log_el = goom_log(jnp.concatenate([A_b, Bu], axis=-2))
        L0I = goom_log(jnp.concatenate([jnp.zeros((d, n), jnp.float32), jnp.eye(n, dtype=jnp.float32)], axis=0))

        def combine(e1, e2):
            aug = jnp.concatenate([e1, jnp.broadcast_to(L0I, e1.shape[:-1] + (n,))], axis=-1)
            return log_matmul_exp(aug, e2)
        log_cum = jax.lax.associative_scan(combine, log_el, axis=1)
        log_x0 = goom_log(init_states)
        log_I = goom_log(jnp.eye(n, dtype=jnp.float32))
        log_x0_I = jnp.concatenate([log_x0, log_I], axis=-1)
        log_x = log_matmul_exp(log_x0_I, log_cum)
        c = jax.lax.stop_gradient(jnp.max(log_x.real, axis=-1, keepdims=True))
        x = jnp.exp(log_x - c + 2).real.reshape(Bsz, L, n * d)
        y = jnp.matmul(x, C) + jnp.matmul(u, D)
        return y

    def _L0_ffn_ref(x, gate_w, biases, w1, w3, w2, sw1, sw3, sw2):
        import jax, jax.numpy as jnp
        import numpy as np
        DIM = 128
        HID = 256
        E = 8
        K = 2
        B, S = (4, 512)
        Bb, Ss, D = x.shape
        xt = x.reshape(Bb * Ss, D)
        shared = jax.nn.silu(xt @ sw1) * (xt @ sw3) @ sw2
        scores = xt @ gate_w.T
        _, idx = jax.lax.top_k(scores + biases, K)
        topv, _ = jax.lax.top_k(scores, K)
        p = jax.nn.sigmoid(topv)
        p = p / jnp.sum(p, axis=-1, keepdims=True)
        h = jax.nn.silu(jnp.einsum('td,edh->eth', xt, w1)) * jnp.einsum('td,edh->eth', xt, w3)
        y = jnp.einsum('eth,ehd->etd', h, w2)
        onehot = jax.nn.one_hot(idx, E, dtype=xt.dtype)
        comb = jnp.einsum('tk,tke->te', p, onehot)
        out = jnp.einsum('te,etd->td', comb, y) + shared
        return out.reshape(Bb, Ss, D)
    h = _L0_tok_ref(x, L0_tok_W, L0_tok_b)
    h = h + _L0_attn_ref(_layernorm(h, axis=-1), L0_attn_init_states, L0_attn_A, L0_attn_B, L0_attn_C, L0_attn_D)
    h = h + _L0_ffn_ref(_layernorm(h, axis=-1), L0_ffn_gate_w, L0_ffn_biases, L0_ffn_w1, L0_ffn_w3, L0_ffn_w2, L0_ffn_sw1, L0_ffn_sw3, L0_ffn_sw2)
    return h

_drawn_inputs = setup_inputs


def setup_inputs(seed=0):
    import zlib

    import numpy as np

    out = dict(_drawn_inputs(seed))
    spreads = {'L0_ffn_biases': (0.0, 0.1)}
    factors = {}
    for name, (base, spread) in spreads.items():
        noise = np.random.default_rng([zlib.crc32(name.encode()), seed]).standard_normal(out[name].shape)
        drawn = base * np.exp(spread * noise) if base else spread * noise
        out[name] = jnp.asarray(drawn.astype(out[name].dtype))
    for name, factor in factors.items():
        out[name] = (out[name] * factor).astype(out[name].dtype)
    return out
```

```python
import math
from contextlib import ExitStack

import concourse.bass as bass
from concourse import mybir

F32 = mybir.dt.float32
BF16 = mybir.dt.bfloat16
I32 = mybir.dt.int32
U32 = mybir.dt.uint32
ALU = mybir.AluOpType
ACT = mybir.ActivationFunctionType
AX_X = mybir.AxisListType.X

P = 128
RING = 4


class Tile:

    def __init__(self, rnd, j, ring=RING):
        self.index = j if isinstance(rnd, int) else rnd * ring + j
        self.slot = j % ring
        self.turn = rnd + j // ring
        self.static = isinstance(rnd, int)


def wait_for(eng, sem, count):
    if isinstance(count, int) and count <= 0:
        return
    eng.wait_ge(sem, count)


def audio_tower_kernel(nc, x, tok_w, tok_b, init_states, a_mat, b_mat, c_mat, d_mat, gate_w, gate_b,
                       w1, w3, w2, sw1, sw3, sw2, out):
    B, T, F = x.shape
    D, PF = tok_w.shape
    HEADS, DH = init_states.shape
    E, _, HID = w1.shape
    STRIDE = PF // F // 2
    CH = STRIDE * F
    L = (T - 2 * STRIDE) // STRIDE + 1
    STEPS = P // B
    TILES = L // STEPS
    NH = CH // P
    NPAIR = HEADS * DH // P
    REGION = TILES * P + P
    RW = P + 4
    XR, WR = 8, 4
    NT = 2 * TILES + E - 1
    TOKENS = TILES * P
    BATCHES = [(k, min(k + 4, TILES)) for k in range(0, TILES, 4)]
    assert D == P and B * STEPS == P and TILES * STEPS == L and CH == NH * P and NPAIR * P == HEADS * DH
    E2 = math.exp(2.0)
    EPS = 1e-5

    with ExitStack() as ctx:
        def sb(name, shape, dt=F32):
            return ctx.enter_context(nc.sbuf_tensor(name, shape, dt))

        def ps(name, shape, dt=F32):
            return ctx.enter_context(nc.psum_tensor(name, shape, dt))

        def sem(name):
            return ctx.enter_context(nc.semaphore(name))

        ident = sb("ident", [P, P])
        iota8 = sb("iota8", [P, E])
        tri = sb("tri", [P, P], BF16)
        ones = sb("ones", [P, P], BF16)
        w_raw = sb("w_raw", [P, PF])
        wT = sb("wT", [P, 2 * NH, P])
        tok_b_bc = sb("tok_b_bc", [P, D])
        gate_b_bc = sb("gate_b_bc", [P, E])
        ad = sb("ad", [P, P])
        adT = sb("adT", [P, P])
        a2d = sb("a2d", [P, P])
        b_sb = sb("b_sb", [P, NPAIR, P])
        bT = sb("bT", [P, NPAIR, P])
        ba = sb("ba", [P, NPAIR, P])
        c_sb = sb("c_sb", [P, NPAIR, D])
        d_sb = sb("d_sb", [P, D])
        gate_raw = sb("gate_raw", [E, D])
        gateT = sb("gateT", [P, E])
        x0 = sb("x0", [P, NPAIR])
        xin = sb("xin", [P, RING, CH])
        xT = sb("xT", [P, RING, NH, P + B])
        u = sb("u", [P, RING, D])
        uT = sb("uT", [P, RING, B + P])
        XT = sb("XT", [P, RING, NPAIR, P])
        xs = sb("xs", [P, NPAIR * P])
        xsT = sb("xsT", [P, NPAIR, P])
        send = sb("send", [P, RING, 2, RW])
        tag_all = sb("tag_all", [P, TILES, 2], I32)
        nT = sb("nT", [P, P])
        h2_all = sb("h2_all", [P, TILES, D])
        nT_all = sb("nT_all", [P, TILES, P])
        stats1 = sb("stats1", [P, 6])
        mom1 = sb("mom1", [P, 2])
        std1 = sb("std1", [P, 1])
        inv1 = sb("inv1", [P, 1])
        stats2 = sb("stats2", [P, 6])
        mom2 = sb("mom2", [P, 2])
        std2 = sb("std2", [P, 1])
        inv2 = sb("inv2", [P, 1])
        shift2 = sb("shift2", [P, 1])
        rowmax = sb("rowmax", [P, HEADS])
        rowinv = sb("rowinv", [P, HEADS])
        biased = sb("biased", [P, E])
        top_b = sb("top_b", [P, 8])
        top_s = sb("top_s", [P, 8])
        top_i = sb("top_i", [P, 8], U32)
        pick_all = sb("pick_all", [P, TILES, 2, E])
        topv_all = sb("topv_all", [P, TILES, 2])
        slot_all = sb("slot_all", [P, TILES, 2])
        oh = sb("oh", [P, E], BF16)
        base = sb("base", [P, E])
        ranked = sb("ranked", [P, E])
        junk = sb("junk", [P, 2, E])
        slot_i = sb("slot_i", [P, RING, 2], I32)
        region_at = sb("region_at", [P, E])
        pad_at = sb("pad_at", [P, E])
        pad_i = sb("pad_i", [P, E], I32)
        pad_row = sb("pad_row", [P, RW])
        tile_no = sb("tile_no", [1, NT])
        upto = sb("upto", [1, E, E])
        cnt_f = sb("cnt_f", [1, E])
        cnt_i = sb("cnt_i", [1, E], I32)
        cnt_s = sb("cnt_s", [1, E], I32)
        ntile = sb("ntile", [1, E])
        ends_m = sb("ends_m", [1, E, E])
        ends = sb("ends", [1, E])
        past = sb("past", [1, NT, E])
        past_n = sb("past_n", [1, NT, E])
        t_exp = sb("t_exp", [1, NT])
        t_first = sb("t_first", [1, NT])
        t_valid = sb("t_valid", [1, NT])
        t_row = sb("t_row", [1, NT])
        t_expv = sb("t_expv", [1, NT])
        table = sb("table", [1, 2, NT], I32)
        sig = sb("sig", [P, TILES, 2])
        sig_sum = sb("sig_sum", [P, TILES])
        sig_inv = sb("sig_inv", [P, TILES])
        prob = sb("prob", [P, TILES, 2])
        sw13 = sb("sw13", [P, 2, HID])
        sw2_sb = sb("sw2_sb", [P, 2, D])
        w13_all = sb("w13_all", [P, E, 2, HID])
        w2_all = sb("w2_all", [P, E, 2, D])
        w13 = sb("w13", [P, WR, 2, HID])
        xg = sb("xg", [P, XR, RW])
        xgT = sb("xgT", [P, XR, P])
        act_h = sb("act_h", [P, 2, 2 * P])
        hid = sb("hid", [P, 2, 2, P])
        yo = sb("yo", [P, XR, D])
        yin = sb("yin", [P, TILES, 2, D])

        xT_ps = ps("xT_ps", [P, NH, P])
        tok_ps = ps("tok_ps", [P, 512])
        uT_ps = ps("uT_ps", [P, 512])
        V_ps = ps("V_ps", [P, NPAIR, 256])
        xtok_ps = ps("xtok_ps", [P, 512])
        xsT_ps = ps("xsT_ps", [P, NPAIR, 256])
        y_ps = ps("y_ps", [P, 512])
        n_ps = ps("n_ps", [P, 512])
        up_ps = (tok_ps, y_ps)
        down_ps = (uT_ps, n_ps)
        rows_ps = (xtok_ps, xT_ps[:, :, :].rearrange("p a b -> p (a b)"))
        xT_ps = xT_ps[:, :, :]
        V = V_ps[:, :, 0:P]
        XSP = xsT_ps[:, :, 0:P]

        routed = nc.dram_tensor("routed", [E * REGION + P, RW], F32, kind="Internal").ap()
        results = nc.dram_tensor("results", [2 * TOKENS, D], F32, kind="Internal").ap()

        names = ("waits_passed w_loaded small_loaded consts_made ad_zeroed x_rest "
                 "set_done set_copied set_vec "
                 "xT_done tok_done uT_done even_done odd_done xtok_done xsT_done y_done nT_done gate_done rank_done "
                 "xT_copied uT_copied even_copied odd_copied xsT_copied nT_copied std1_ready std2_ready "
                 "h_ready stats1_ready mom1_ready inv1_ready u_ready rowmax_ready rowinv_ready xs_ready "
                 "h2_ready stats2_ready mom2_ready inv2_ready xn_ready shift2_ready tag_copied "
                 "biased_ready topv_ready scores_read top_ready topi_ready pick_ready oh_ready "
                 "ranked_ready rank_read pickrank_ready slot_copied slots_ready out_stored "
                 "ffn_loaded spare_padded pads_ready padded tables_made table_ready sig_ready prob_ready "
                 "sup_done sact_ready shid_ready sout_done sadded up_done act_ready hid_ready out_done yo_ready "
                 "xgT_done xgT_copied mid_ready fin_ready").split()
        S = type("S", (), {n: sem(n) for n in names})
        sent_back = [sem(f"sent_back{i}") for i in range(XR)]
        xg_loaded = [sem(f"xg_loaded{i}") for i in range(XR)]
        w13_loaded = [sem(f"w13_loaded{i}") for i in range(WR)]
        yin_loaded = [sem(f"yin_loaded{n}") for n in range(len(BATCHES))]
        x_loaded = [sem(f"x_loaded{i}") for i in range(RING)]
        scattered = [sem(f"scattered{i}") for i in range(RING)]

        chunks = x[:, 0:TILES * STEPS * STRIDE, :].rearrange("b (k c s) f -> k c b (s f)", c=STEPS, s=STRIDE)
        last_chunk = x[:, L * STRIDE:(L + 1) * STRIDE, :].rearrange("b s f -> b (s f)")
        CONSTS = 18
        TOWER_LOOP = (RING, 2, 5, 2)
        EXPERT_LOOP = (XR, 1, NT // XR - 1, 0)
        SHARED_LOOP = (RING, 1, TILES // RING, 0)
        block = ctx.enter_context(nc.Block())

        def run_steps(eng, step, last, loop=TOWER_LOOP):
            ring, first, end, shift = loop
            for s in range(first * ring + shift):
                step(0, s)
            with eng.Fori(first, end) as rnd:
                for s in range(shift, shift + ring):
                    step(rnd, s)
            for s in range(end * ring + shift, last + 1):
                step(0, s)

        def wait_alone(eng, sem, count):
            wait_for(eng, sem, count)
            if not isinstance(count, int):
                eng.sem_inc(S.waits_passed, 1)

        def tile(rnd, s, lag, tiles=TILES, ring=RING):
            if isinstance(rnd, int) and not 0 <= s - lag < tiles:
                return None
            return Tile(rnd, s - lag, ring)

        @block.sync
        def _(sp):
            def load(t):
                if not t.static or t.index >= RING:
                    wait_for(sp, S.xT_done, t.index - RING + 1)
                sp.dma_start(xin[:, t.slot, :], chunks[t.index]).then_inc(x_loaded[t.slot], 16)

            load(Tile(0, 0))
            sp.dma_start(w_raw[:], tok_w).then_inc(S.w_loaded, 16)
            load(Tile(0, 1))
            for hp in range(2):
                sp.wait_ge(S.ad_zeroed, 1)
                sp.dma_start(ad[hp * DH:(hp + 1) * DH, hp * DH:(hp + 1) * DH], a_mat).then_inc(S.small_loaded, 16)
            sp.dma_start(b_sb[:, :, :], b_mat.rearrange("d (q m) -> d q m", q=NPAIR)).then_inc(S.small_loaded, 16)
            sp.dma_start(gate_raw[:], gate_w).then_inc(S.small_loaded, 16)
            sp.dma_start(x0[:], init_states.rearrange("h d -> (h d)").rearrange("(q p) -> p q", p=P), allow_slow_non_contiguous=True).then_inc(S.small_loaded, 16)
            sp.dma_start(tok_b_bc[:], tok_b.unsqueeze(0).to_broadcast([P, D])).then_inc(S.small_loaded, 16)
            sp.dma_start(gate_b_bc[:], gate_b.unsqueeze(0).to_broadcast([P, E])).then_inc(S.small_loaded, 16)
            sp.dma_start(c_sb[:, :, :], c_mat.rearrange("(q p) d -> p q d", p=P)).then_inc(S.small_loaded, 16)
            sp.dma_start(d_sb[:], d_mat).then_inc(S.small_loaded, 16)
            load(Tile(0, 2))
            load(Tile(0, 3))
            with sp.Fori(1, TILES // RING) as rnd:
                for s in range(RING):
                    load(Tile(rnd, s))
            for s in range(TILES // RING * RING, TILES):
                load(Tile(0, s))
            t = Tile(0, TILES)
            sp.wait_ge(S.xT_done, t.index - RING + 1)
            sp.dma_start(xin[0:B, t.slot, :], last_chunk).then_inc(x_loaded[t.slot], 16)
            sp.dma_start(sw13[:, 0, :], sw1).then_inc(S.ffn_loaded, 16)
            sp.dma_start(sw13[:, 1, :], sw3).then_inc(S.ffn_loaded, 16)
            sp.dma_start(sw2_sb[:, :, :], sw2.rearrange("(q p) d -> p q d", p=P)).then_inc(S.ffn_loaded, 16)
            sp.dma_start(w13_all[:, :, 0, :], w1.rearrange("e p h -> p e h")).then_inc(S.ffn_loaded, 16)
            sp.dma_start(w13_all[:, :, 1, :], w3.rearrange("e p h -> p e h")).then_inc(S.ffn_loaded, 16)
            for q in range(2):
                sp.dma_start(w2_all[:, :, q, :], w2[:, q * P:(q + 1) * P, :].rearrange("e p d -> p e d")).then_inc(S.ffn_loaded, 16)
            sp.wait_ge(S.consts_made, CONSTS)
            sp.dma_start(routed[E * REGION:E * REGION + P, :], pad_row[:]).then_inc(S.spare_padded, 16)

            sp.wait_ge(S.table_ready, 1)
            sp.wait_ge(S.ffn_loaded, 16 * 7)
            for r in range(RING):
                sp.wait_ge(scattered[r], 32 * len(range(r, TILES, RING)))
            sp.wait_ge(S.padded, 16 * E)
            sp.wait_ge(S.spare_padded, 16)

            def step(rnd, s):
                t = Tile(rnd, s, XR)
                entry = sp.value_load(table[0:1, 0, bass.ds(t.index, 1)], min_val=0, max_val=E * REGION * E + E - 1)
                row, e = entry // E, entry % E
                if not t.static or t.index >= XR:
                    wait_alone(sp, sent_back[t.slot], t.turn * 16)
                    wait_for(sp, S.xgT_done, t.index - XR + 1)
                sp.dma_start(xg[:, t.slot, :], routed[bass.ds(row, P), :]).then_inc(xg_loaded[t.slot], 16)
                if not t.static or t.index >= WR:
                    wait_for(sp, S.up_done, t.index - WR + 1)
                sp.dma_start(w13[:, t.slot % WR, :, :], w13_all[:, bass.ds(e, 1), :, :].rearrange("p a w h -> p (a w) h")).then_inc(w13_loaded[t.slot % WR], 16)
            run_steps(sp, step, NT - 1, EXPERT_LOOP)
            for r in range(XR):
                sp.wait_ge(sent_back[r], 16 * len(range(r, NT, XR)))

            by_tile = results.rearrange("(k p j) d -> p k j d", p=P, j=2)
            for n, (k0, k1) in enumerate(BATCHES):
                sp.dma_start(yin[:, k0:k1, :, :], by_tile[:, k0:k1, :, :]).then_inc(yin_loaded[n], 16)

        @block.gpsimd
        def _(pool):
            pool.memset(ad[:], 0.0).then_inc(S.ad_zeroed, 1)
            pool.memset(ident[:], 0.0).then_inc(S.consts_made, 1)
            pool.memset(tri[:], 1.0).then_inc(S.consts_made, 1)
            pool.memset(ones[:], 1.0).then_inc(S.consts_made, 1)
            pool.iota(iota8[:], [[1, E]], base=0, channel_multiplier=0, allow_small_or_imprecise_dtypes=True).then_inc(S.consts_made, 1)
            pool.iota(base[:], [[REGION, E]], base=0, channel_multiplier=0, allow_small_or_imprecise_dtypes=True).then_inc(S.consts_made, 1)
            pool.memset(uT[:, 0, 0:B], 0.0).then_inc(S.consts_made, 1)
            pool.memset(XT[:, RING - 1, :, :], 0.0).then_inc(S.consts_made, 1)
            pool.iota(tag_all[:, :, :], [[2 * P, TILES], [1, 2]], base=0, channel_multiplier=2).then_inc(S.consts_made, 1)
            pool.iota(pad_at[:, :], [[0, E]], base=0, channel_multiplier=1, allow_small_or_imprecise_dtypes=True).then_inc(S.consts_made, 1)
            pool.iota(tile_no[:], [[1, NT]], base=0, channel_multiplier=0, allow_small_or_imprecise_dtypes=True).then_inc(S.consts_made, 1)
            pool.iota(region_at[:], [[REGION, E]], base=0, channel_multiplier=0, allow_small_or_imprecise_dtypes=True).then_inc(S.consts_made, 1)
            pool.memset(upto[:, :, :], 1.0).then_inc(S.consts_made, 1)
            pool.memset(pad_row[:], 0.0).then_inc(S.consts_made, 1)
            pool.memset(send[:, :, :, D:RW], 0.0).then_inc(S.consts_made, 1)
            pool.wait_ge(S.consts_made, 14)
            pool.iota(pad_row[:, D:D + 1].bitcast(I32), [[0, 1]], base=2 * TOKENS, channel_multiplier=0).then_inc(S.consts_made, 1)
            pool.affine_select(out=upto[:, :, :], in_=upto[:, :, :], compare_op=ALU.is_ge, fill=0.0, base=0,
                               pattern=[[1, E], [-1, E]], channel_multiplier=0).then_inc(S.consts_made, 1)
            pool.affine_select(out=ident[:], in_=ident[:], compare_op=ALU.not_equal, fill=1.0, base=0,
                               pattern=[[-1, P]], channel_multiplier=1).then_inc(S.consts_made, 1)
            pool.affine_select(out=tri[:], in_=tri[:], compare_op=ALU.is_gt, fill=0.0, base=0,
                               pattern=[[1, P]], channel_multiplier=-1).then_inc(S.consts_made, 1)

            def step(rnd, s):
                if t := tile(rnd, s, 0):
                    if not t.static or t.index >= RING:
                        wait_for(pool, scattered[t.slot], t.turn * 32)
                    pool.tensor_copy(send[:, t.slot, :, D:D + 1].bitcast(I32),
                                     tag_all[:, bass.ds(t.index, 1), :].rearrange("p a j -> p j a")).then_inc(S.tag_copied, 1)
                    wait_for(pool, S.tag_copied, t.index + 1)
                    wait_for(pool, S.slots_ready, t.index + 1)
                    pool.tensor_copy(slot_i[:, t.slot, :], slot_all[:, bass.ds(t.index, 1), :].rearrange("p a j -> p (a j)")).then_inc(S.slot_copied, 1)
                    wait_for(pool, S.slot_copied, t.index + 1)
                    wait_alone(pool, S.xn_ready, 2 * t.index + 2)
                    for j in range(2):
                        pool.indirect_dma_start(out=routed, out_offset=bass.IndirectOffsetOnAxis(ap=slot_i[:, t.slot, j:j + 1], axis=0),
                                                in_=send[:, t.slot, j, :], in_offset=None).then_inc(scattered[t.slot], 16)
            run_steps(pool, step, TILES - 1, SHARED_LOOP)
            pool.wait_ge(S.pads_ready, 1)
            for e in range(E):
                pool.indirect_dma_start(out=routed, out_offset=bass.IndirectOffsetOnAxis(ap=pad_i[:, e:e + 1], axis=0),
                                        in_=pad_row[:], in_offset=None).then_inc(S.padded, 16)

            def step(rnd, s):
                if t := tile(rnd, s, 1, NT, XR):
                    wait_alone(pool, S.yo_ready, t.index + 1)
                    pool.indirect_dma_start(out=results, out_offset=bass.IndirectOffsetOnAxis(ap=xg[:, t.slot, D:D + 1].bitcast(I32), axis=0),
                                            in_=yo[:, t.slot, :], in_offset=None, bounds_check=2 * TOKENS - 1,
                                            oob_is_err=False).then_inc(sent_back[t.slot], 16)
            run_steps(pool, step, NT, EXPERT_LOOP)



        @block.tensor
        def _(pe):
            pe.wait_ge(S.consts_made, CONSTS)
            pe.wait_ge(S.w_loaded, 16)
            for q in range(2 * NH):
                ins = pe.transpose(tok_ps[:, q * P:(q + 1) * P], w_raw[:, q * P:(q + 1) * P], ident[:])
            ins.then_inc(S.set_done, 1)

            def prepare():
                pe.wait_ge(S.small_loaded, 16 * 9)
                pe.transpose(y_ps[:, 0:P], ad[:], ident[:])
                for q in range(NPAIR):
                    pe.transpose(y_ps[:, (1 + q) * P:(2 + q) * P], b_sb[:, q, :], ident[:])
                pe.transpose(y_ps[:, 3 * P:3 * P + E], gate_raw[:], ident[0:E, 0:E]).then_inc(S.set_done, 1)
                pe.wait_ge(S.set_copied, 3)
                pe.matmul(y_ps[:, 0:P], adT[:], ad[:], start=True, stop=True)
                for q in range(NPAIR):
                    ins = pe.matmul(y_ps[:, (1 + q) * P:(2 + q) * P], bT[:, q, :], ad[:], start=True, stop=True)
                ins.then_inc(S.set_done, 1)

            def step(rnd, s):
                if t := tile(rnd, s, 3):
                    wait_for(pe, S.uT_copied, t.index + 1)
                    wait_for(pe, S.odd_copied, t.index)
                    if t.static and t.index == 0:
                        pe.wait_ge(S.set_copied, 4)
                    for q in range(NPAIR):
                        pe.matmul(V[:, q, :], b_sb[:, q, :], uT[:, t.slot, B:B + P], start=q == 0, stop=False, skip_group_check=True)
                    for q in range(NPAIR):
                        pe.matmul(V[:, q, :], ba[:, q, :], uT[:, t.slot, 0:P], start=False, stop=False, skip_group_check=True)
                    prev = (t.slot - 1) % RING
                    if t.static and t.index == 0:
                        pe.wait_ge(S.set_vec, 1)
                        pe.matmul(V[:, :, 0:B], ad[:], XT[:, prev, :, P - B:P], start=False, stop=False, skip_group_check=True)
                    pe.matmul(V[:, :, 0:P // 2], a2d[:], XT[:, prev, :, P // 2:P], start=False, stop=False,
                              skip_group_check=True).then_inc(S.even_done, 1)
                if t := tile(rnd, s, 5):
                    wait_for(pe, S.xs_ready, t.index + 1)
                    wait_for(pe, S.xsT_copied, t.index)
                    for q in range(NPAIR):
                        ins = pe.transpose(XSP[:, q, :], xs[:, q * P:(q + 1) * P], ident[:])
                    ins.then_inc(S.xsT_done, 1)
                if t := tile(rnd, s, 4):
                    wait_for(pe, S.odd_copied, t.index + 1)
                    wait_for(pe, S.xs_ready, t.index)
                    for q in range(NPAIR):
                        ins = pe.transpose(xtok_ps[:, q * P:(q + 1) * P], XT[:, t.slot, q, :], ident[:])
                    ins.then_inc(S.xtok_done, 1)
                if t := tile(rnd, s, 8):
                    wait_for(pe, S.oh_ready, t.index + 1)
                    wait_for(pe, S.uT_copied, min(t.index + 6, TILES) if t.static else t.index + 6)
                    pe.matmul(uT_ps[:, P:P + E], tri[:], oh[:], start=True, stop=True)
                    pe.matmul(uT_ps[:, P + E:P + 2 * E], ones[:], oh[:], start=True, stop=True).then_inc(S.rank_done, 1)
                if t := tile(rnd, s, 7):
                    wait_for(pe, S.nT_copied, t.index + 1)
                    pe.matmul(n_ps[:, 2 * P:2 * P + E], nT[:], gateT[:], start=True, stop=True).then_inc(S.gate_done, 1)
                if t := tile(rnd, s, 1):
                    wait_for(pe, S.xT_copied, t.index + 2)
                    wait_for(pe, S.h_ready, t.index)
                    if t.static and t.index == 0:
                        pe.wait_ge(S.set_copied, 1)
                    for q in range(2 * NH):
                        off = (q // NH) * B
                        ins = pe.matmul(tok_ps[:, 0:D], xT[:, t.slot, q % NH, off:off + P], wT[:, q, :], start=q == 0, stop=q == 2 * NH - 1)
                    ins.then_inc(S.tok_done, 1)
                if t := tile(rnd, s, 3):
                    wait_for(pe, S.even_copied, t.index + 1)
                    pe.matmul(V[:, :, P // 2:P], a2d[:], XT[:, t.slot, :, 0:P // 2], start=False, stop=True,
                              skip_group_check=True).then_inc(S.odd_done, 1)
                if t := tile(rnd, s, 5):
                    wait_for(pe, S.xsT_copied, t.index + 1)
                    wait_for(pe, S.h2_ready, t.index)
                    for q in range(NPAIR):
                        pe.matmul(y_ps[:, 0:D], xsT[:, q, :], c_sb[:, q, :], start=q == 0, stop=False)
                    pe.matmul(y_ps[:, 0:D], uT[:, t.slot, B:B + P], d_sb[:], start=False, stop=True).then_inc(S.y_done, 1)
                if t := tile(rnd, s, 2):
                    wait_for(pe, S.u_ready, t.index + 1)
                    wait_for(pe, S.rank_read, t.index - 5)
                    pe.transpose(uT_ps[:, 0:P], u[:, t.slot, :], ident[:]).then_inc(S.uT_done, 1)
                if t := tile(rnd, s, -1, TILES + 1):
                    transpose_x(t)
                if t := tile(rnd, s, 6):
                    wait_for(pe, S.xn_ready, 2 * t.index + 1)
                    wait_for(pe, S.scores_read, t.index)
                    pe.transpose(n_ps[:, 0:P], send[:, t.slot, 0, 0:D], ident[:]).then_inc(S.nT_done, 1)

            def transpose_x(t):
                last = t.static and t.index == TILES
                wait_for(pe, x_loaded[t.slot], (t.turn + 1) * 16)
                wait_for(pe, S.xT_copied, t.index)
                rows = B if last else P
                for q in range(NH):
                    ins = pe.transpose(xT_ps[:, q, 0:rows], xin[0:rows, t.slot, q * P:(q + 1) * P], ident[0:rows, 0:rows])
                ins.then_inc(S.xT_done, 1)

            transpose_x(Tile(0, 0))
            prepare()
            run_steps(pe, step, TILES + 7)

            for sm in (S.h_ready, S.h2_ready, S.xs_ready, S.scores_read, S.rank_read):
                pe.wait_ge(sm, TILES)
            pe.wait_ge(S.ffn_loaded, 16 * 7)

            def up(ps_bank, weights, xT_ap):
                for w in range(2):
                    for q in range(2):
                        at = (2 * w + q) * P
                        ins = pe.matmul(ps_bank[:, at:at + P], weights[:, w, q * P:(q + 1) * P], xT_ap, start=True, stop=True)
                return ins

            def step(rnd, s):
                if t := tile(rnd, s, 0):
                    if not t.static or t.index >= 2:
                        wait_for(pe, S.shid_ready, t.index - 1)
                    up(up_ps[t.slot % 2], sw13, nT_all[:, bass.ds(t.index, 1), :].rearrange("p a n -> p (a n)")).then_inc(S.sup_done, 1)
                if t := tile(rnd, s, 1):
                    wait_for(pe, S.shid_ready, t.index + 1)
                    wait_for(pe, S.sadded, t.index - 1)
                    for q in range(2):
                        ins = pe.matmul(down_ps[t.slot % 2][:, 0:D], hid[:, t.slot % 2, q, :], sw2_sb[:, q, :], start=q == 0, stop=q == 1)
                    ins.then_inc(S.sout_done, 1)
            run_steps(pe, step, TILES, SHARED_LOOP)

            pe.wait_ge(S.sadded, TILES)

            def transpose_rows(t):
                wait_for(pe, xg_loaded[t.slot], (t.turn + 1) * 16)
                wait_for(pe, S.xgT_copied, t.index - 1)
                pe.transpose(rows_ps[t.slot % 2][:, 0:P], xg[:, t.slot, 0:D], ident[:]).then_inc(S.xgT_done, 1)

            def step(rnd, s):
                if t := tile(rnd, s, 0, NT, XR):
                    wait_for(pe, w13_loaded[t.slot % WR], (t.turn * (XR // WR) + t.slot // WR + 1) * 16)
                    wait_for(pe, S.xgT_copied, t.index + 1)
                    wait_for(pe, S.hid_ready, t.index - 1)
                    up(up_ps[t.slot % 2], w13[:, t.slot % WR], xgT[:, t.slot, :]).then_inc(S.up_done, 1)
                if tile(rnd, s, 1, NT, XR):
                    t = tile(rnd, s, 1, NT, XR)
                    e = pe.value_load(table[0:1, 1, bass.ds(t.index, 1)], min_val=0, max_val=E - 1)
                if t := tile(rnd, s, -2, NT, XR):
                    transpose_rows(t)
                if t := tile(rnd, s, 1, NT, XR):
                    wait_for(pe, S.hid_ready, t.index + 1)
                    wait_for(pe, S.yo_ready, t.index - 1)
                    for q in range(2):
                        ins = pe.matmul(down_ps[t.slot % 2][:, 0:D], hid[:, t.slot % 2, q, :],
                                        w2_all[:, bass.ds(e, 1), q, :].rearrange("p a d -> p (a d)"), start=q == 0, stop=q == 1)
                    ins.then_inc(S.out_done, 1)
            transpose_rows(Tile(0, 0, XR))
            transpose_rows(Tile(0, 1, XR))
            run_steps(pe, step, NT, EXPERT_LOOP)

        @block.scalar
        def _(act):
            def copy(o, i, scale=1.0):
                return act.activation(o, i, ACT.Copy, scale=scale)

            act.wait_ge(S.set_done, 1)
            copy(wT[:, :, :], tok_ps[:, :].rearrange("p (q d) -> p q d", q=2 * NH)).then_inc(S.set_copied, 1)
            act.wait_ge(S.set_done, 2)
            copy(adT[:], y_ps[:, 0:P])
            copy(gateT[:], y_ps[:, 3 * P:3 * P + E]).then_inc(S.set_copied, 1)
            copy(bT[:, :, :], y_ps[:, P:3 * P].rearrange("p (q d) -> p q d", q=NPAIR)).then_inc(S.set_copied, 1)
            act.wait_ge(S.set_done, 3)
            copy(a2d[:], y_ps[:, 0:P])
            copy(ba[:, :, :], y_ps[:, P:3 * P].rearrange("p (q d) -> p q d", q=NPAIR)).then_inc(S.set_copied, 1)

            def copy_xT(t):
                wait_for(act, S.xT_done, t.index + 1)
                if t.static and t.index == TILES:
                    copy(xT[:, (t.slot - 1) % RING, :, P:P + B], xT_ps[:, :, 0:B]).then_inc(S.xT_copied, 1)
                    return
                ins = copy(xT[:, t.slot, :, 0:P], xT_ps)
                if not t.static or t.index > 0:
                    ins = copy(xT[:, (t.slot - 1) % RING, :, P:P + B], xT_ps[:, :, 0:B])
                ins.then_inc(S.xT_copied, 1)

            def step(rnd, s):
                if t := tile(rnd, s, 3):
                    wait_for(act, S.even_done, t.index + 1)
                    copy(XT[:, t.slot, :, 0:P // 2], V[:, :, 0:P // 2]).then_inc(S.even_copied, 1)
                if t := tile(rnd, s, 5):
                    wait_for(act, S.xsT_done, t.index + 1)
                    copy(xsT[:, :, :], XSP, scale=E2).then_inc(S.xsT_copied, 1)
                if t := tile(rnd, s, 2):
                    wait_for(act, S.mom1_ready, t.index + 1)
                    act.activation(std1[:], mom1[:, 1:2], ACT.Sqrt, bias=EPS).then_inc(S.std1_ready, 1)
                if t := tile(rnd, s, 6):
                    wait_for(act, S.mom2_ready, t.index + 1)
                    act.activation(std2[:], mom2[:, 1:2], ACT.Sqrt, bias=EPS).then_inc(S.std2_ready, 1)
                if t := tile(rnd, s, 3):
                    wait_for(act, S.odd_done, t.index + 1)
                    copy(XT[:, t.slot, :, P // 2:P], V[:, :, P // 2:P]).then_inc(S.odd_copied, 1)
                if t := tile(rnd, s, 2):
                    wait_for(act, S.uT_done, t.index + 1)
                    copy(uT[:, t.slot, B:B + P], uT_ps[:, 0:P])
                    copy(uT[:, (t.slot + 1) % RING, 0:B], uT_ps[:, P - B:P]).then_inc(S.uT_copied, 1)
                if t := tile(rnd, s, -1, TILES + 1):
                    copy_xT(t)
                if t := tile(rnd, s, 6):
                    wait_for(act, S.shift2_ready, t.index + 1)
                    if not t.static or t.index >= RING:
                        wait_for(act, scattered[t.slot], t.turn * 32)
                    h2 = h2_all[:, bass.ds(t.index, 1), :].rearrange("p a d -> p (a d)")
                    act.activation(send[:, t.slot, 0, 0:D], h2, ACT.Identity, bias=shift2[:], scale=inv2[:]).then_inc(S.xn_ready, 1)
                    act.activation(send[:, t.slot, 1, 0:D], h2, ACT.Identity, bias=shift2[:], scale=inv2[:]).then_inc(S.xn_ready, 1)
                if t := tile(rnd, s, 6):
                    wait_for(act, S.nT_done, t.index + 1)
                    copy(nT[:], n_ps[:, 0:P])
                    copy(nT_all[:, bass.ds(t.index, 1), :].rearrange("p a d -> p (a d)"), n_ps[:, 0:P]).then_inc(S.nT_copied, 1)

            copy_xT(Tile(0, 0))
            run_steps(act, step, TILES + 5)

            act.wait_ge(S.topv_ready, TILES)
            act.activation(sig[:, :, :], topv_all[:, :, :], ACT.Sigmoid).then_inc(S.sig_ready, 1)

            def step(rnd, s):
                if t := tile(rnd, s, 0):
                    wait_for(act, S.sup_done, t.index + 1)
                    if not t.static or t.index >= 2:
                        wait_for(act, S.shid_ready, t.index - 1)
                    act.activation(act_h[:, t.slot % 2, :], up_ps[t.slot % 2][:, 0:2 * P], ACT.Silu).then_inc(S.sact_ready, 1)
            run_steps(act, step, TILES - 1, SHARED_LOOP)

            def copy_rows(t):
                wait_for(act, S.xgT_done, t.index + 1)
                copy(xgT[:, t.slot, :], rows_ps[t.slot % 2][:, 0:P]).then_inc(S.xgT_copied, 1)

            def step(rnd, s):
                if t := tile(rnd, s, 0, NT, XR):
                    wait_for(act, S.up_done, t.index + 1)
                    wait_for(act, S.hid_ready, t.index - 1)
                    act.activation(act_h[:, t.slot % 2, :], up_ps[t.slot % 2][:, 0:2 * P], ACT.Silu).then_inc(S.act_ready, 1)
                if t := tile(rnd, s, -2, NT, XR):
                    copy_rows(t)
                if t := tile(rnd, s, 1, NT, XR):
                    wait_for(act, S.out_done, t.index + 1)
                    if not t.static or t.index >= XR:
                        wait_for(act, sent_back[t.slot], t.turn * 16)
                    copy(yo[:, t.slot, :], down_ps[t.slot % 2][:, 0:D]).then_inc(S.yo_ready, 1)
            copy_rows(Tile(0, 0, XR))
            copy_rows(Tile(0, 1, XR))
            run_steps(act, step, NT, EXPERT_LOOP)

            out_tiles = out.rearrange("b (k c) d -> c b k d", c=STEPS)
            for n, (k0, k1) in enumerate(BATCHES):
                act.wait_ge(S.fin_ready, n + 1)
                for c in range(STEPS):
                    act.dma_start(out_tiles[c, :, k0:k1, :], h2_all[c * B:(c + 1) * B, k0:k1, :]).then_inc(S.out_stored, 16)
            act.wait_ge(S.out_stored, 16 * STEPS * len(BATCHES))

        @block.vector
        def _(dve):
            dve.wait_ge(S.consts_made, CONSTS)
            dve.wait_ge(S.small_loaded, 16 * 9)
            for q in range(NPAIR):
                ins = dve.tensor_copy(XT[:, RING - 1, q, P - B:P], x0[:, q:q + 1].to_broadcast([P, B]))
            ins.then_inc(S.set_vec, 1)

            def step(rnd, s):
                ln1, ln2, srt, cho, mx = (tile(rnd, s, lag) for lag in (2, 6, 8, 7, 4))
                if t := ln1:
                    h1 = h2_all[:, bass.ds(t.index, 1), :].rearrange("p a d -> p (a d)")
                    wait_for(dve, S.tok_done, t.index + 1)
                    dve.tensor_tensor(h1, tok_ps[:, 0:D], tok_b_bc[:], ALU.add).then_inc(S.h_ready, 1)
                if t := ln2:
                    h2 = h2_all[:, bass.ds(t.index, 1), :].rearrange("p a d -> p (a d)")
                    wait_for(dve, S.y_done, t.index + 1)
                    dve.tensor_tensor(h2, y_ps[:, 0:D], h2, ALU.add).then_inc(S.h2_ready, 1)
                if t := ln1:
                    wait_alone(dve, S.h_ready, t.index + 1)
                    dve.bn_stats(stats1[:], h1).then_inc(S.stats1_ready, 1)
                if t := ln2:
                    wait_alone(dve, S.h2_ready, t.index + 1)
                    dve.bn_stats(stats2[:], h2).then_inc(S.stats2_ready, 1)
                if t := ln1:
                    wait_alone(dve, S.stats1_ready, t.index + 1)
                    dve.bn_aggr(mom1[:], stats1[:]).then_inc(S.mom1_ready, 1)
                if t := ln2:
                    wait_alone(dve, S.stats2_ready, t.index + 1)
                    dve.bn_aggr(mom2[:], stats2[:]).then_inc(S.mom2_ready, 1)
                if t := mx:
                    wait_for(dve, S.xtok_done, t.index + 1)
                    xh = xtok_ps[:, 0:NPAIR * P].rearrange("p (h d) -> p h d", h=HEADS)
                    dve.tensor_reduce(rowmax[:], xh, AX_X, ALU.max, apply_absolute_value=True).then_inc(S.rowmax_ready, 1)
                if t := ln1:
                    wait_for(dve, S.std1_ready, t.index + 1)
                    dve.reciprocal(inv1[:], std1[:]).then_inc(S.inv1_ready, 1)
                if t := ln2:
                    wait_for(dve, S.std2_ready, t.index + 1)
                    dve.reciprocal(inv2[:], std2[:]).then_inc(S.inv2_ready, 1)
                if t := ln1:
                    wait_for(dve, S.inv1_ready, t.index + 1)
                    dve.tensor_scalar(u[:, t.slot, :], h1, mom1[:, 0:1], inv1[:, 0:1], ALU.subtract, ALU.mult).then_inc(S.u_ready, 1)
                if t := ln2:
                    wait_for(dve, S.inv2_ready, t.index + 1)
                    dve.tensor_scalar(shift2[:], mom2[:, 0:1], inv2[:, 0:1], -1.0, ALU.mult, ALU.mult).then_inc(S.shift2_ready, 1)
                if t := srt:
                    wait_for(dve, S.rank_done, t.index + 1)
                    wait_for(dve, S.rank_read, t.index)
                    dve.tensor_tensor(ranked[:], uT_ps[:, P:P + E], base[:], ALU.add).then_inc(S.ranked_ready, 1)
                    dve.tensor_tensor(base[:], base[:], uT_ps[:, P + E:P + 2 * E], ALU.add).then_inc(S.rank_read, 1)
                if t := cho:
                    wait_for(dve, S.gate_done, t.index + 1)
                    dve.tensor_tensor(biased[:], n_ps[:, 2 * P:2 * P + E], gate_b_bc[:], ALU.add).then_inc(S.biased_ready, 1)
                    dve.max(top_s[:], n_ps[:, 2 * P:2 * P + E]).then_inc(S.scores_read, 1)
                if t := srt:
                    wait_for(dve, S.ranked_ready, t.index + 1)
                    pick = pick_all[:, bass.ds(t.index, 1), :, :].rearrange("p a j e -> p (a j) e")
                    dve.tensor_tensor(junk[:, :, :], pick, ranked[:].unsqueeze(1).to_broadcast([P, 2, E]), ALU.mult).then_inc(S.pickrank_ready, 1)
                if t := cho:
                    wait_alone(dve, S.biased_ready, t.index + 1)
                    dve.max(top_b[:], biased[:]).then_inc(S.top_ready, 1)
                    wait_alone(dve, S.scores_read, t.index + 1)
                    topv = topv_all[:, bass.ds(t.index, 1), :].rearrange("p a j -> p (a j)")
                    dve.tensor_copy(topv, top_s[:, 0:2]).then_inc(S.topv_ready, 1)
                if t := srt:
                    wait_for(dve, S.pickrank_ready, t.index + 1)
                    slots = slot_all[:, bass.ds(t.index, 1), :].rearrange("p a j -> p (a j)")
                    dve.tensor_reduce(slots, junk[:, :, :], AX_X, ALU.add).then_inc(S.slots_ready, 1)
                if t := cho:
                    wait_alone(dve, S.top_ready, t.index + 1)
                    dve.max_index(top_i[:], top_b[:], biased[:]).then_inc(S.topi_ready, 1)
                if t := mx:
                    wait_for(dve, S.rowmax_ready, t.index + 1)
                    dve.reciprocal(rowinv[:], rowmax[:]).then_inc(S.rowinv_ready, 1)
                if t := cho:
                    wait_alone(dve, S.topi_ready, t.index + 1)
                    pick = pick_all[:, bass.ds(t.index, 1), :, :].rearrange("p a j e -> p (a j) e")
                    dve.tensor_tensor(pick, iota8[:].unsqueeze(1).to_broadcast([P, 2, E]),
                                      top_i[:, 0:2].unsqueeze(2).to_broadcast([P, 2, E]), ALU.is_equal).then_inc(S.pick_ready, 1)
                if t := mx:
                    wait_for(dve, S.rowinv_ready, t.index + 1)
                    dve.tensor_tensor(xs[:].rearrange("p (h d) -> p h d", h=HEADS), xh,
                                      rowinv[:].unsqueeze(2).to_broadcast([P, HEADS, DH]), ALU.mult).then_inc(S.xs_ready, 1)
                if t := cho:
                    wait_for(dve, S.pick_ready, t.index + 1)
                    dve.tensor_tensor(oh[:], pick[:, 0, :], pick[:, 1, :], ALU.add).then_inc(S.oh_ready, 1)

            run_steps(dve, step, TILES + 7)

            dve.wait_ge(S.rank_read, TILES)
            dve.tensor_tensor(pad_i[:], base[:], pad_at[:], ALU.add).then_inc(S.pads_ready, 1)

            made = 0

            def link(ins):
                nonlocal made
                made += 1
                ins.then_inc(S.tables_made, 1)
                dve.wait_ge(S.tables_made, made)

            def over(ap, n):
                return ap.unsqueeze(1).to_broadcast([1, n, E])

            link(dve.tensor_tensor(cnt_f[:], base[0:1, :], region_at[0:1, :], ALU.subtract))
            link(dve.tensor_scalar(cnt_i[:], cnt_f[:], float(P - 1), None, ALU.add))
            link(dve.tensor_scalar(cnt_s[:], cnt_i[:], P.bit_length() - 1, None, ALU.arith_shift_right))
            link(dve.tensor_copy(ntile[:], cnt_s[:]))
            link(dve.tensor_tensor(ends_m[:, :, :], upto[:, :, :], over(ntile[:], E), ALU.mult))
            link(dve.tensor_reduce(ends[:], ends_m[:, :, :], AX_X, ALU.add))
            link(dve.tensor_tensor(past[:, :, :], tile_no[:].unsqueeze(2).to_broadcast([1, NT, E]), over(ends[:], NT), ALU.is_ge))
            link(dve.tensor_reduce(t_exp[:], past[:, :, :], AX_X, ALU.add))
            link(dve.tensor_tensor(past_n[:, :, :], past[:, :, :], over(ntile[:], NT), ALU.mult))
            link(dve.tensor_reduce(t_first[:], past_n[:, :, :], AX_X, ALU.add))
            link(dve.tensor_tensor(t_row[:], tile_no[:], t_first[:], ALU.subtract))
            link(dve.tensor_scalar(t_valid[:], t_exp[:], float(E), float(P), ALU.is_lt, ALU.mult))
            link(dve.tensor_tensor(t_row[:], t_row[:], t_valid[:], ALU.mult))
            link(dve.scalar_tensor_tensor(out=t_row[:], in0=t_exp[:], scalar=float(REGION), in1=t_row[:], op0=ALU.mult, op1=ALU.add))
            link(dve.tensor_scalar(t_expv[:], t_exp[:], float(E - 1), None, ALU.min))
            link(dve.tensor_copy(table[:, 1, :], t_expv[:]))
            dve.scalar_tensor_tensor(out=table[:, 0, :], in0=t_row[:], scalar=float(E), in1=t_expv[:], op0=ALU.mult, op1=ALU.add).then_inc(S.table_ready, 1)

            dve.wait_ge(S.sig_ready, 1)
            link(dve.tensor_tensor(sig_sum[:], sig[:, :, 0], sig[:, :, 1], ALU.add))
            link(dve.reciprocal(sig_inv[:], sig_sum[:]))
            dve.tensor_tensor(prob[:, :, :], sig[:, :, :], sig_inv[:].unsqueeze(2).to_broadcast([P, TILES, 2]), ALU.mult).then_inc(S.prob_ready, 1)

            def gate_hidden(t, read, done):
                dve.tensor_tensor(hid[:, t.slot % 2, :, :].rearrange("p q n -> p (q n)"), act_h[:, t.slot % 2, :],
                                  up_ps[t.slot % 2][:, 2 * P:4 * P], ALU.mult).then_inc(done, 1)

            def step(rnd, s):
                if t := tile(rnd, s, 0):
                    wait_for(dve, S.sact_ready, t.index + 1)
                    wait_for(dve, S.sout_done, t.index - 1)
                    gate_hidden(t, None, S.shid_ready)
                if t := tile(rnd, s, 1):
                    wait_for(dve, S.sout_done, t.index + 1)
                    h2 = h2_all[:, bass.ds(t.index, 1), :].rearrange("p a d -> p (a d)")
                    dve.tensor_tensor(h2, down_ps[t.slot % 2][:, 0:D], h2, ALU.add).then_inc(S.sadded, 1)
            run_steps(dve, step, TILES, SHARED_LOOP)

            def step(rnd, s):
                t = Tile(rnd, s, XR)
                wait_for(dve, S.act_ready, t.index + 1)
                wait_for(dve, S.out_done, t.index - 1)
                gate_hidden(t, None, S.hid_ready)
            run_steps(dve, step, NT - 1, EXPERT_LOOP)

            dve.wait_ge(S.prob_ready, 1)
            dve.wait_ge(S.sadded, TILES)

            for n, (k0, k1) in enumerate(BATCHES):
                dve.wait_ge(yin_loaded[n], 16)
                for k in range(k0, k1):
                    dve.scalar_tensor_tensor(out=h2_all[:, k, :], in0=yin[:, k, 0, :], scalar=prob[:, k, 0:1], in1=h2_all[:, k, :],
                                             op0=ALU.mult, op1=ALU.add).then_inc(S.mid_ready, 1)
                for k in range(k0, k1):
                    dve.wait_ge(S.mid_ready, k + 1)
                    ins = dve.scalar_tensor_tensor(out=h2_all[:, k, :], in0=yin[:, k, 1, :], scalar=prob[:, k, 1:2], in1=h2_all[:, k, :],
                                                   op0=ALU.mult, op1=ALU.add)
                ins.then_inc(S.fin_ready, 1)


_INS = ["x", "L0_tok_W", "L0_tok_b", "L0_attn_init_states", "L0_attn_A", "L0_attn_B", "L0_attn_C", "L0_attn_D",
        "L0_ffn_gate_w", "L0_ffn_biases", "L0_ffn_w1", "L0_ffn_w3", "L0_ffn_w2", "L0_ffn_sw1", "L0_ffn_sw3", "L0_ffn_sw2"]
_OUT = ((32, 92, 128), "float32")


def kernel(**inputs):
    import numpy as _np
    import concourse.bacc as _bacc
    from concourse import mybir as _mybir
    from concourse.bass_utils import run_bass_kernel_spmd as _run

    nc = _bacc.Bacc("TRN2", target_bir_lowering=False, num_devices=1)
    arrays, args = {}, []
    for name in _INS:
        a = _np.ascontiguousarray(inputs[name])
        arrays[f"in_{name}_dram"] = a
        args.append(nc.dram_tensor(f"in_{name}_dram", a.shape, _mybir.dt.from_np(a.dtype), kind="ExternalInput").ap())
    shape, dtype = _OUT
    args.append(nc.dram_tensor("out_dram", shape, _mybir.dt.from_np(_np.dtype(dtype)), kind="ExternalOutput").ap())
    audio_tower_kernel(nc, *args)
    r = _run(nc, [arrays], core_ids=[0])
    return r.results[0]["out_dram"]
```

```python
import math
from contextlib import ExitStack

import concourse.bass as bass
from concourse import mybir

F32 = mybir.dt.float32
BF16 = mybir.dt.bfloat16
I32 = mybir.dt.int32
U32 = mybir.dt.uint32
ALU = mybir.AluOpType
ACT = mybir.ActivationFunctionType
AX_X = mybir.AxisListType.X

P = 128
RING = 4


class Tile:

    def __init__(self, rnd, j, ring=RING):
        self.index = j if isinstance(rnd, int) else rnd * ring + j
        self.slot = j % ring
        self.turn = rnd + j // ring
        self.static = isinstance(rnd, int)


def wait_for(eng, sem, count):
    if isinstance(count, int) and count <= 0:
        return
    eng.wait_ge(sem, count)


def audio_tower_kernel(nc, x, tok_w, tok_b, init_states, a_mat, b_mat, c_mat, d_mat, gate_w, gate_b,
                       w1, w3, w2, sw1, sw3, sw2, out):
    B, T, F = x.shape
    D, PF = tok_w.shape
    HEADS, DH = init_states.shape
    E, _, HID = w1.shape
    STRIDE = PF // F // 2
    CH = STRIDE * F
    L = (T - 2 * STRIDE) // STRIDE + 1
    STEPS = P // B
    TILES = L // STEPS
    NH = CH // P
    NPAIR = HEADS * DH // P
    REGION = 1 << (TILES * P + 2 * P - 1).bit_length()
    RTILES = REGION // P
    RW = P + 4
    XR = 8
    NT = 2 * TILES + E - 1
    TOKENS = TILES * P
    COLS = -(-(NT + 2) // XR) * XR
    SPLIT = TILES * 16 // 23
    DVE_LOADS = [(0, SPLIT // 4), (SPLIT // 4, SPLIT // 2), (SPLIT // 2, SPLIT)]
    POOL_LOADS = [(SPLIT, (SPLIT + TILES) // 2), ((SPLIT + TILES) // 2, TILES)]
    DVE_STORES = [(0, SPLIT // 2), (SPLIT // 2, SPLIT)]
    POOL_STORES = [(SPLIT, TILES)]
    assert D == P and B * STEPS == P and TILES * STEPS == L and CH == NH * P and NPAIR * P == HEADS * DH
    E2 = math.exp(2.0)
    EPS = 1e-5

    with ExitStack() as ctx:
        def sb(name, shape, dt=F32):
            return ctx.enter_context(nc.sbuf_tensor(name, shape, dt))

        def ps(name, shape, dt=F32):
            return ctx.enter_context(nc.psum_tensor(name, shape, dt))

        def sem(name):
            return ctx.enter_context(nc.semaphore(name))

        ident = sb("ident", [P, P])
        iota8 = sb("iota8", [P, E])
        tri = sb("tri", [P, P], BF16)
        ones = sb("ones", [P, P], BF16)
        w_raw = sb("w_raw", [P, PF])
        wT = sb("wT", [P, 2 * NH, P])
        tok_b_bc = sb("tok_b_bc", [P, D])
        gate_b_bc = sb("gate_b_bc", [P, E])
        ad = sb("ad", [P, P])
        adT = sb("adT", [P, P])
        a2d = sb("a2d", [P, P])
        b_sb = sb("b_sb", [P, NPAIR, P])
        bT = sb("bT", [P, NPAIR, P])
        ba = sb("ba", [P, NPAIR, P])
        c_sb = sb("c_sb", [P, NPAIR, D])
        d_sb = sb("d_sb", [P, D])
        gate_raw = sb("gate_raw", [E, D])
        gateT = sb("gateT", [P, E])
        x0 = sb("x0", [P, NPAIR])
        xin = sb("xin", [P, RING, CH])
        xT = sb("xT", [P, RING, NH, P + B])
        u = sb("u", [P, RING, D])
        uT = sb("uT", [P, RING, B + P])
        XT = sb("XT", [P, RING, NPAIR, P])
        xs = sb("xs", [P, NPAIR * P])
        xsT = sb("xsT", [P, NPAIR, P])
        send = sb("send", [P, RING, 2, RW])
        tag_all = sb("tag_all", [P, TILES, 2], I32)
        nT = sb("nT", [P, P])
        h2_all = sb("h2_all", [P, TILES, D])
        nT_all = sb("nT_all", [P, TILES, P])
        stats1 = sb("stats1", [P, 6])
        mom1 = sb("mom1", [P, 2])
        warm = sb("warm", [P, 1])
        std1 = sb("std1", [P, 1])
        inv1 = sb("inv1", [P, 1])
        stats2 = sb("stats2", [P, 6])
        mom2 = sb("mom2", [P, 2])
        std2 = sb("std2", [P, 1])
        inv2 = sb("inv2", [P, 1])
        shift2 = sb("shift2", [P, 1])
        rowmax = sb("rowmax", [P, HEADS])
        rowinv = sb("rowinv", [P, HEADS])
        biased = sb("biased", [P, E])
        top_b = sb("top_b", [P, 8])
        top_s = sb("top_s", [P, RING, 8])
        top_i = sb("top_i", [P, 8], U32)
        pick_all = sb("pick_all", [P, TILES, 2, E])
        topv_all = sb("topv_all", [P, TILES, 2])
        slot_all = sb("slot_all", [P, TILES, 2])
        oh = sb("oh", [P, E], BF16)
        base = sb("base", [P, E])
        ranked = sb("ranked", [P, E])
        junk = sb("junk", [P, 2, E])
        slot_i = sb("slot_i", [P, RING, 2], I32)
        region_at = sb("region_at", [P, E])
        pad_at = sb("pad_at", [P, E])
        pad_i = sb("pad_i", [P, E], I32)
        pad_row = sb("pad_row", [P, RW])
        tile_no = sb("tile_no", [1, COLS])
        upto = sb("upto", [1, E, E])
        cnt_f = sb("cnt_f", [1, E])
        cnt_i = sb("cnt_i", [1, E], I32)
        cnt_s = sb("cnt_s", [1, E], I32)
        ntile = sb("ntile", [1, E])
        ends_m = sb("ends_m", [1, E, E])
        ends = sb("ends", [1, E])
        past = sb("past", [1, COLS, E])
        past_n = sb("past_n", [1, COLS, E])
        t_exp = sb("t_exp", [1, COLS])
        t_first = sb("t_first", [1, COLS])
        t_valid = sb("t_valid", [1, COLS])
        t_row = sb("t_row", [1, COLS])
        e_pair = sb("e_pair", [1, COLS // 2])
        e_four = sb("e_four", [1, COLS // 4])
        row_words = sb("row_words", [1, COLS // 2 - 1], I32)
        expert_words = sb("expert_words", [1, COLS // 8], I32)
        sig = sb("sig", [P, TILES, 2])
        sig_sum = sb("sig_sum", [P, TILES])
        sig_inv = sb("sig_inv", [P, TILES])
        prob = sb("prob", [P, TILES, 2])
        sw13 = sb("sw13", [P, 2, HID])
        sw2_sb = sb("sw2_sb", [P, 2, D])
        w13_all = sb("w13_all", [P, E, 2 * HID])
        w2_all = sb("w2_all", [P, E, 2, D])
        xg = sb("xg", [P, XR, RW])
        xgT = sb("xgT", [P, XR, P])
        act_h = sb("act_h", [P, 2, 2 * P])
        hid = sb("hid", [P, 2, 2, P])
        hidT = sb("hidT", [P, 2, 2, P])
        yo = sb("yo", [P, XR, D])
        yin = sb("yin", [P, TILES, 2, D])

        xT_ps = ps("xT_ps", [P, NH, P])
        tok_ps = ps("tok_ps", [P, 512])
        uT_ps = ps("uT_ps", [P, 512])
        V_ps = ps("V_ps", [P, NPAIR, 256])
        xtok_ps = ps("xtok_ps", [P, 512])
        xsT_ps = ps("xsT_ps", [P, NPAIR, 256])
        y_ps = ps("y_ps", [P, 512])
        n_ps = ps("n_ps", [P, 512])
        up_ps = (tok_ps, y_ps)
        down_ps = (uT_ps, n_ps)
        rows_ps = (xtok_ps, xT_ps[:, :, :].rearrange("p a b -> p (a b)"))
        xT_ps = xT_ps[:, :, :]
        hidT_ps = (V_ps[:, :, :].rearrange("p a b -> p (a b)"), xsT_ps[:, :, :].rearrange("p a b -> p (a b)"))
        V = V_ps[:, :, 0:P]
        XSP = xsT_ps[:, :, 0:P]

        routed = nc.dram_tensor("routed", [E * REGION, RW], F32, kind="Internal").ap()
        results = nc.dram_tensor("results", [2 * TOKENS, D], F32, kind="Internal").ap()

        names = ("waits_passed w_loaded tok_b_loaded small_loaded late_loaded table_warm consts_made ad_zeroed "
                 "set_done set_copied set_vec "
                 "xT_done tok_done uT_done even_done odd_done xtok_done xsT_done y_done nT_done gate_done rank_done "
                 "xT_copied uT_copied even_copied odd_copied xsT_copied nT_copied std1_ready std2_ready "
                 "h_ready stats1_ready mom1_ready inv1_ready u_ready rowmax_ready rowinv_ready xs_ready "
                 "h2_ready stats2_ready mom2_ready inv2_ready xn_ready xn_twice shift2_ready tag_copied "
                 "biased_ready topv_ready scores_read top_ready topi_ready pick_ready oh_ready "
                 "ranked_ready rank_read pickrank_ready slot_copied slots_ready out_stored "
                 "ffn_loaded spare_padded pads_ready padded tables_made table_ready sig_ready prob_ready "
                 "sup_done sact_ready shid_ready sout_done sadded up_done act_ready hid_ready hidT_done hidT_copied out_done yo_ready "
                 "xgT_done xgT_copied mid_ready fin_ready pool_mid_ready pool_fin_ready pool_out_stored").split()
        S = type("S", (), {n: sem(n) for n in names})
        sent_back = [sem(f"sent_back{i}") for i in range(XR)]
        xg_loaded = [sem(f"xg_loaded{i}") for i in range(XR)]
        yin_loaded = {span: sem(f"yin_loaded{span[0]}") for span in DVE_LOADS + POOL_LOADS}
        x_loaded = [sem(f"x_loaded{i}") for i in range(RING)]
        scattered = [sem(f"scattered{i}") for i in range(RING)]

        chunks = x[:, 0:TILES * STEPS * STRIDE, :].rearrange("b (k c s) f -> k c b (s f)", c=STEPS, s=STRIDE)
        last_chunk = x[:, L * STRIDE:(L + 1) * STRIDE, :].rearrange("b s f -> b (s f)")
        CONSTS = 18
        ROW_RADIX = RTILES * E
        TOWER_LOOP = (RING, 2, 5, 2)
        EXPERT_LOOP = (XR, 1, NT // XR - 1, 0)
        SHARED_LOOP = (RING, 1, TILES // RING, 0)
        block = ctx.enter_context(nc.Block())

        def run_steps(eng, step, last, loop=TOWER_LOOP, start=0):
            ring, first, end, shift = loop
            for s in range(start, first * ring + shift):
                step(0, s)
            with eng.Fori(first, end) as rnd:
                for s in range(shift, shift + ring):
                    step(rnd, s)
            for s in range(end * ring + shift, last + 1):
                step(0, s)

        def wait_alone(eng, sem, count):
            wait_for(eng, sem, count)
            if not isinstance(count, int):
                eng.sem_inc(S.waits_passed, 1)

        def tile(rnd, s, lag, tiles=TILES, ring=RING):
            if isinstance(rnd, int) and not 0 <= s - lag < tiles:
                return None
            return Tile(rnd, s - lag, ring)

        def store(eng, spans, ready, first, stored):
            count = 0
            for k0, k1 in spans:
                eng.wait_ge(ready, k1 - first)
                if k1 - k0 == 1:
                    eng.dma_start(out.rearrange("b (k c) d -> k c b d", c=STEPS)[k0], h2_all[:, k0, :]).then_inc(stored, 16)
                    count += 1
                    continue
                for c in range(STEPS):
                    eng.dma_start(out.rearrange("b (k c) d -> c b k d", c=STEPS)[c, :, k0:k1, :],
                                  h2_all[c * B:(c + 1) * B, k0:k1, :]).then_inc(stored, 16)
                count += STEPS
            eng.wait_ge(stored, 16 * count)

        @block.sync
        def _(sp):
            def load(t):
                if not t.static or t.index >= RING:
                    wait_for(sp, S.xT_done, t.index - RING + 1)
                sp.dma_start(xin[:, t.slot, :], chunks[t.index]).then_inc(x_loaded[t.slot], 16)

            load(Tile(0, 0))
            sp.dma_start(w_raw[:], tok_w).then_inc(S.w_loaded, 16)
            load(Tile(0, 1))
            sp.dma_start(tok_b_bc[:], tok_b.unsqueeze(0).to_broadcast([P, D])).then_inc(S.tok_b_loaded, 16)
            load(Tile(0, 2))
            sp.wait_ge(S.ad_zeroed, 1)
            for hp in range(2):
                sp.dma_start(ad[hp * DH:(hp + 1) * DH, hp * DH:(hp + 1) * DH], a_mat).then_inc(S.small_loaded, 16)
            sp.dma_start(b_sb[:, :, :], b_mat.rearrange("d (q m) -> d q m", q=NPAIR)).then_inc(S.small_loaded, 16)
            sp.dma_start(gate_raw[:], gate_w).then_inc(S.small_loaded, 16)
            sp.dma_start(x0[:], init_states.rearrange("h d -> (h d)").rearrange("(q p) -> p q", p=P), allow_slow_non_contiguous=True).then_inc(S.small_loaded, 16)
            load(Tile(0, 3))
            sp.dma_start(gate_b_bc[:], gate_b.unsqueeze(0).to_broadcast([P, E])).then_inc(S.late_loaded, 16)
            sp.dma_start(c_sb[:, :, :], c_mat.rearrange("(q p) d -> p q d", p=P)).then_inc(S.late_loaded, 16)
            sp.dma_start(d_sb[:], d_mat).then_inc(S.late_loaded, 16)
            with sp.Fori(1, TILES // RING) as rnd:
                for s in range(RING):
                    load(Tile(rnd, s))
            for s in range(TILES // RING * RING, TILES):
                load(Tile(0, s))
            t = Tile(0, TILES)
            sp.wait_ge(S.xT_done, t.index - RING + 1)
            sp.dma_start(xin[0:B, t.slot, :], last_chunk).then_inc(x_loaded[t.slot], 16)
            sp.dma_start(sw13[:, 0, :], sw1).then_inc(S.ffn_loaded, 16)
            sp.dma_start(sw13[:, 1, :], sw3).then_inc(S.ffn_loaded, 16)
            sp.dma_start(sw2_sb[:, :, :], sw2.rearrange("(q p) d -> p q d", p=P)).then_inc(S.ffn_loaded, 16)
            sp.dma_start(w13_all[:, :, 0:HID], w1.rearrange("e p h -> p e h")).then_inc(S.ffn_loaded, 16)
            sp.dma_start(w13_all[:, :, HID:2 * HID], w3.rearrange("e p h -> p e h")).then_inc(S.ffn_loaded, 16)
            for q in range(2):
                sp.dma_start(w2_all[:, :, q, :], w2[:, q * P:(q + 1) * P, :].rearrange("e p d -> p e d")).then_inc(S.ffn_loaded, 16)
            sp.wait_ge(S.consts_made, CONSTS)
            sp.dma_start(routed[E * REGION - P:E * REGION, :], pad_row[:]).then_inc(S.spare_padded, 16)

            picked = [0, 0]
            sp.wait_ge(S.table_ready, 2)
            sp.wait_ge(S.ffn_loaded, 16 * 7)
            for r in range(RING):
                sp.wait_ge(scattered[r], 32 * len(range(r, TILES, RING)))
            sp.wait_ge(S.padded, 16 * E)
            sp.wait_ge(S.spare_padded, 16)

            def step(rnd, s):
                t = Tile(rnd, s, XR)
                if t.slot % 2 == 0:
                    pair = sp.value_load(row_words[0:1, bass.ds(t.turn * (XR // 2) + t.slot // 2, 1)], min_val=0, max_val=ROW_RADIX ** 2 - 1)
                    picked[:] = [pair % ROW_RADIX, pair // ROW_RADIX]
                row = picked[t.slot % 2] * P
                if not t.static or t.index >= XR:
                    wait_alone(sp, sent_back[t.slot], t.turn * 16)
                    wait_for(sp, S.xgT_done, t.index - XR + 1)
                sp.dma_start(xg[:, t.slot, :], routed[bass.ds(row, P), :]).then_inc(xg_loaded[t.slot], 16)
            run_steps(sp, step, NT - 1, EXPERT_LOOP)
            for r in range(XR):
                sp.wait_ge(sent_back[r], 16 * len(range(r, NT, XR)))

            by_tile = results.rearrange("(k p j) d -> p k j d", p=P, j=2)
            for k0, k1 in (DVE_LOADS[0], POOL_LOADS[0], DVE_LOADS[1], DVE_LOADS[2], POOL_LOADS[1]):
                sp.dma_start(yin[:, k0:k1, :, :], by_tile[:, k0:k1, :, :]).then_inc(yin_loaded[k0, k1], 16)
            store(sp, POOL_STORES, S.pool_fin_ready, SPLIT, S.pool_out_stored)

        @block.gpsimd
        def _(pool):
            pool.memset(ad[:], 0.0).then_inc(S.ad_zeroed, 1)
            pool.memset(ident[:], 0.0).then_inc(S.consts_made, 1)
            pool.memset(tri[:], 1.0).then_inc(S.consts_made, 1)
            pool.memset(ones[:], 1.0).then_inc(S.consts_made, 1)
            pool.iota(iota8[:], [[1, E]], base=0, channel_multiplier=0, allow_small_or_imprecise_dtypes=True).then_inc(S.consts_made, 1)
            pool.iota(base[:], [[REGION, E]], base=0, channel_multiplier=0, allow_small_or_imprecise_dtypes=True).then_inc(S.consts_made, 1)
            pool.memset(uT[:, 0, 0:B], 0.0).then_inc(S.consts_made, 1)
            pool.memset(XT[:, RING - 1, :, :], 0.0).then_inc(S.consts_made, 1)
            pool.iota(tag_all[:, :, :], [[2 * P, TILES], [1, 2]], base=0, channel_multiplier=2).then_inc(S.consts_made, 1)
            pool.iota(pad_at[:, :], [[0, E]], base=0, channel_multiplier=1, allow_small_or_imprecise_dtypes=True).then_inc(S.consts_made, 1)
            pool.iota(tile_no[:], [[1, COLS]], base=-2, channel_multiplier=0, allow_small_or_imprecise_dtypes=True).then_inc(S.consts_made, 1)
            pool.iota(region_at[:], [[REGION, E]], base=0, channel_multiplier=0, allow_small_or_imprecise_dtypes=True).then_inc(S.consts_made, 1)
            pool.memset(upto[:, :, :], 1.0).then_inc(S.consts_made, 1)
            pool.memset(pad_row[:], 0.0).then_inc(S.consts_made, 1)
            pool.memset(send[:, :, :, D:RW], 0.0).then_inc(S.consts_made, 1)
            pool.wait_ge(S.consts_made, 14)
            pool.iota(pad_row[:, D:D + 1].bitcast(I32), [[0, 1]], base=2 * TOKENS, channel_multiplier=0).then_inc(S.consts_made, 1)
            pool.affine_select(out=upto[:, :, :], in_=upto[:, :, :], compare_op=ALU.is_ge, fill=0.0, base=0,
                               pattern=[[1, E], [-1, E]], channel_multiplier=0).then_inc(S.consts_made, 1)
            pool.affine_select(out=ident[:], in_=ident[:], compare_op=ALU.not_equal, fill=1.0, base=0,
                               pattern=[[-1, P]], channel_multiplier=1).then_inc(S.consts_made, 1)
            pool.affine_select(out=tri[:], in_=tri[:], compare_op=ALU.is_gt, fill=0.0, base=0,
                               pattern=[[1, P]], channel_multiplier=-1).then_inc(S.consts_made, 1)

            def step(rnd, s):
                if t := tile(rnd, s, 0):
                    if not t.static or t.index >= RING:
                        wait_for(pool, scattered[t.slot], t.turn * 32)
                    pool.tensor_copy(send[:, t.slot, :, D:D + 1].bitcast(I32),
                                     tag_all[:, bass.ds(t.index, 1), :].rearrange("p a j -> p j a")).then_inc(S.tag_copied, 1)
                    wait_alone(pool, S.xn_ready, t.index + 1)
                    pool.tensor_copy(send[:, t.slot, 1, 0:D], send[:, t.slot, 0, 0:D]).then_inc(S.xn_twice, 1)
                    wait_alone(pool, S.scores_read, t.index + 1)
                    pool.tensor_copy(topv_all[:, bass.ds(t.index, 1), :].rearrange("p a j -> p (a j)"), top_s[:, t.slot, 0:2]).then_inc(S.topv_ready, 1)
                    wait_for(pool, S.tag_copied, t.index + 1)
                    wait_for(pool, S.slots_ready, t.index + 1)
                    pool.tensor_copy(slot_i[:, t.slot, :], slot_all[:, bass.ds(t.index, 1), :].rearrange("p a j -> p (a j)")).then_inc(S.slot_copied, 1)
                    wait_for(pool, S.slot_copied, t.index + 1)
                    wait_alone(pool, S.xn_twice, t.index + 1)
                    for j in range(2):
                        pool.indirect_dma_start(out=routed, out_offset=bass.IndirectOffsetOnAxis(ap=slot_i[:, t.slot, j:j + 1], axis=0),
                                                in_=send[:, t.slot, j, :], in_offset=None).then_inc(scattered[t.slot], 16)
            run_steps(pool, step, TILES - 1, SHARED_LOOP)
            pool.wait_ge(S.pads_ready, 1)
            for e in range(E):
                pool.indirect_dma_start(out=routed, out_offset=bass.IndirectOffsetOnAxis(ap=pad_i[:, e:e + 1], axis=0),
                                        in_=pad_row[:], in_offset=None).then_inc(S.padded, 16)

            def step(rnd, s):
                if t := tile(rnd, s, 1, NT, XR):
                    wait_alone(pool, S.yo_ready, t.index + 1)
                    pool.indirect_dma_start(out=results, out_offset=bass.IndirectOffsetOnAxis(ap=xg[:, t.slot, D:D + 1].bitcast(I32), axis=0),
                                            in_=yo[:, t.slot, :], in_offset=None, bounds_check=2 * TOKENS - 1,
                                            oob_is_err=False).then_inc(sent_back[t.slot], 16)
            run_steps(pool, step, NT, EXPERT_LOOP)

            pool.wait_ge(S.prob_ready, 1)
            pool.wait_ge(S.sadded, TILES)
            steps_done = 0
            for k0, k1 in POOL_LOADS:
                y2, h2 = yin[:, k0:k1, :, :], h2_all[:, k0:k1, :]
                pool.wait_ge(yin_loaded[k0, k1], 16)
                pool.tensor_tensor(y2, y2, prob[:, k0:k1, :].unsqueeze(3).to_broadcast([P, k1 - k0, 2, D]), ALU.mult).then_inc(S.pool_mid_ready, 1)
                pool.wait_ge(S.pool_mid_ready, steps_done + 1)
                pool.tensor_tensor(yin[:, k0:k1, 0, :], yin[:, k0:k1, 0, :], yin[:, k0:k1, 1, :], ALU.add).then_inc(S.pool_mid_ready, 1)
                pool.wait_ge(S.pool_mid_ready, steps_done + 2)
                pool.tensor_tensor(h2, yin[:, k0:k1, 0, :], h2, ALU.add).then_inc(S.pool_fin_ready, k1 - k0)
                steps_done += 2

        @block.tensor
        def _(pe):
            pe.wait_ge(S.consts_made, CONSTS)
            pe.wait_ge(S.w_loaded, 16)
            for q in range(2 * NH):
                ins = pe.transpose(tok_ps[:, q * P:(q + 1) * P], w_raw[:, q * P:(q + 1) * P], ident[:])
            ins.then_inc(S.set_done, 1)

            def prepare():
                pe.wait_ge(S.small_loaded, 16 * 5)
                pe.transpose(y_ps[:, 0:P], ad[:], ident[:])
                for q in range(NPAIR):
                    pe.transpose(y_ps[:, (1 + q) * P:(2 + q) * P], b_sb[:, q, :], ident[:])
                pe.transpose(y_ps[:, 3 * P:3 * P + E], gate_raw[:], ident[0:E, 0:E]).then_inc(S.set_done, 1)
                pe.wait_ge(S.set_copied, 3)
                pe.matmul(y_ps[:, 0:P], adT[:], ad[:], start=True, stop=True)
                for q in range(NPAIR):
                    ins = pe.matmul(y_ps[:, (1 + q) * P:(2 + q) * P], bT[:, q, :], ad[:], start=True, stop=True)
                ins.then_inc(S.set_done, 1)

            def step(rnd, s):
                if t := tile(rnd, s, 5):
                    wait_for(pe, S.xs_ready, t.index + 1)
                    wait_for(pe, S.xsT_copied, t.index)
                    for q in range(NPAIR):
                        ins = pe.transpose(XSP[:, q, :], xs[:, q * P:(q + 1) * P], ident[:])
                    ins.then_inc(S.xsT_done, 1)
                if t := tile(rnd, s, 4):
                    wait_for(pe, S.odd_copied, t.index + 1)
                    wait_for(pe, S.xs_ready, t.index)
                    for q in range(NPAIR):
                        ins = pe.transpose(xtok_ps[:, q * P:(q + 1) * P], XT[:, t.slot, q, :], ident[:])
                    ins.then_inc(S.xtok_done, 1)
                if t := tile(rnd, s, 3):
                    wait_for(pe, S.uT_copied, t.index + 1)
                    wait_for(pe, S.odd_copied, t.index)
                    if t.static and t.index == 0:
                        pe.wait_ge(S.set_copied, 4)
                    for q in range(NPAIR):
                        pe.matmul(V[:, q, :], b_sb[:, q, :], uT[:, t.slot, B:B + P], start=q == 0, stop=False, skip_group_check=True)
                    for q in range(NPAIR):
                        pe.matmul(V[:, q, :], ba[:, q, :], uT[:, t.slot, 0:P], start=False, stop=False, skip_group_check=True)
                    prev = (t.slot - 1) % RING
                    if t.static and t.index == 0:
                        pe.wait_ge(S.set_vec, 1)
                        pe.matmul(V[:, :, 0:B], ad[:], XT[:, prev, :, P - B:P], start=False, stop=False, skip_group_check=True)
                    pe.matmul(V[:, :, 0:P // 2], a2d[:], XT[:, prev, :, P // 2:P], start=False, stop=False,
                              skip_group_check=True).then_inc(S.even_done, 1)
                if t := tile(rnd, s, 7):
                    wait_for(pe, S.xn_ready, t.index + 1)
                    wait_for(pe, S.scores_read, t.index)
                    pe.transpose(n_ps[:, 0:P], send[:, t.slot, 0, 0:D], ident[:]).then_inc(S.nT_done, 1)
                if t := tile(rnd, s, 8):
                    wait_for(pe, S.oh_ready, t.index + 1)
                    wait_for(pe, S.uT_copied, min(t.index + 6, TILES) if t.static else t.index + 6)
                    pe.matmul(uT_ps[:, P:P + E], tri[:], oh[:], start=True, stop=True)
                    pe.matmul(uT_ps[:, P + E:P + 2 * E], ones[:], oh[:], start=True, stop=True).then_inc(S.rank_done, 1)
                if t := tile(rnd, s, 1):
                    wait_for(pe, S.xT_copied, t.index + 2)
                    wait_for(pe, S.h_ready, t.index)
                    if t.static and t.index == 0:
                        pe.wait_ge(S.set_copied, 1)
                    for q in range(2 * NH):
                        off = (q // NH) * B
                        ins = pe.matmul(tok_ps[:, 0:D], xT[:, t.slot, q % NH, off:off + P], wT[:, q, :], start=q == 0, stop=q == 2 * NH - 1)
                    ins.then_inc(S.tok_done, 1)
                if t := tile(rnd, s, 7):
                    wait_for(pe, S.nT_copied, t.index + 1)
                    pe.matmul(n_ps[:, 2 * P:2 * P + E], nT[:], gateT[:], start=True, stop=True).then_inc(S.gate_done, 1)
                if t := tile(rnd, s, 3):
                    wait_for(pe, S.even_copied, t.index + 1)
                    pe.matmul(V[:, :, P // 2:P], a2d[:], XT[:, t.slot, :, 0:P // 2], start=False, stop=True,
                              skip_group_check=True).then_inc(S.odd_done, 1)
                if t := tile(rnd, s, 2):
                    wait_for(pe, S.u_ready, t.index + 1)
                    wait_for(pe, S.rank_read, t.index - 5)
                    pe.transpose(uT_ps[:, 0:P], u[:, t.slot, :], ident[:]).then_inc(S.uT_done, 1)
                if t := tile(rnd, s, 5):
                    wait_for(pe, S.xsT_copied, t.index + 1)
                    wait_for(pe, S.h2_ready, t.index)
                    if t.static and t.index == 0:
                        pe.wait_ge(S.late_loaded, 16 * 3)
                    for q in range(NPAIR):
                        pe.matmul(y_ps[:, 0:D], xsT[:, q, :], c_sb[:, q, :], start=q == 0, stop=False)
                    pe.matmul(y_ps[:, 0:D], uT[:, t.slot, B:B + P], d_sb[:], start=False, stop=True).then_inc(S.y_done, 1)
                if t := tile(rnd, s, -1, TILES + 1):
                    transpose_x(t)

            def transpose_x(t):
                last = t.static and t.index == TILES
                wait_for(pe, x_loaded[t.slot], (t.turn + 1) * 16)
                wait_for(pe, S.xT_copied, t.index)
                rows = B if last else P
                for q in range(NH):
                    ins = pe.transpose(xT_ps[:, q, 0:rows], xin[0:rows, t.slot, q * P:(q + 1) * P], ident[0:rows, 0:rows])
                ins.then_inc(S.xT_done, 1)

            transpose_x(Tile(0, 0))
            step(0, 0)
            step(0, 1)
            prepare()
            run_steps(pe, step, TILES + 7, start=2)

            for sm in (S.h_ready, S.h2_ready, S.xs_ready, S.scores_read, S.rank_read):
                pe.wait_ge(sm, TILES)
            pe.wait_ge(S.ffn_loaded, 16 * 7)

            def up(ps_bank, weights, xT_ap):
                for w in range(2):
                    for q in range(2):
                        at = (2 * w + q) * P
                        ins = pe.matmul(ps_bank[:, at:at + P], weights[:, w, q * P:(q + 1) * P], xT_ap, start=True, stop=True)
                return ins

            def step(rnd, s):
                if t := tile(rnd, s, 0):
                    if not t.static or t.index >= 2:
                        wait_for(pe, S.shid_ready, t.index - 1)
                    up(up_ps[t.slot % 2], sw13, nT_all[:, bass.ds(t.index, 1), :].rearrange("p a n -> p (a n)")).then_inc(S.sup_done, 1)
                if t := tile(rnd, s, 1):
                    wait_for(pe, S.shid_ready, t.index + 1)
                    wait_for(pe, S.sadded, t.index - 1)
                    for q in range(2):
                        ins = pe.matmul(down_ps[t.slot % 2][:, 0:D], hid[:, t.slot % 2, q, :], sw2_sb[:, q, :], start=q == 0, stop=q == 1)
                    ins.then_inc(S.sout_done, 1)
            run_steps(pe, step, TILES, SHARED_LOOP)

            pe.wait_ge(S.sadded, TILES)

            def transpose_rows(t):
                wait_for(pe, xg_loaded[t.slot], (t.turn + 1) * 16)
                wait_for(pe, S.xgT_copied, t.index - 1)
                pe.transpose(rows_ps[t.slot % 2][:, 0:P], xg[:, t.slot, 0:D], ident[:]).then_inc(S.xgT_done, 1)

            def load_word(t):
                return pe.value_load(expert_words[0:1, bass.ds(t.turn, 1)], min_val=0, max_val=E ** XR - 1)

            def expert(t, in_word):
                return in_word // E ** ((t.slot + 2) % XR) % E

            def step(rnd, s):
                now = Tile(rnd, s, XR)
                if now.slot == 0:
                    words[:] = [load_word(now)] * 2
                if now.slot == XR - 2 and tile(rnd, s, 0, NT, XR):
                    words[0] = load_word(Tile(rnd, s + 2, XR))
                if t := tile(rnd, s, 0, NT, XR):
                    wait_for(pe, S.xgT_copied, t.index + 1)
                    wait_for(pe, S.hid_ready, t.index - 1)
                    pe.matmul(up_ps[t.slot % 2][:, :], xgT[:, t.slot, :], w13_all[:, bass.ds(expert(t, words[0]), 1), :].rearrange("p a h -> p (a h)"),
                              start=True, stop=True).then_inc(S.up_done, 1)
                if t := tile(rnd, s, 1, NT, XR):
                    wait_for(pe, S.hid_ready, t.index + 1)
                    wait_for(pe, S.hidT_copied, t.index - 1)
                    for q in range(2):
                        ins = pe.transpose(hidT_ps[t.slot % 2][:, q * P:(q + 1) * P], hid[:, t.slot % 2, q, :], ident[:])
                    ins.then_inc(S.hidT_done, 1)
                if t := tile(rnd, s, -2, NT, XR):
                    transpose_rows(t)
                if t := tile(rnd, s, 2, NT, XR):
                    wait_for(pe, S.hidT_copied, t.index + 1)
                    wait_for(pe, S.yo_ready, t.index - 1)
                    for q in range(2):
                        ins = pe.matmul(down_ps[t.slot % 2][:, 0:D], hidT[:, t.slot % 2, q, :],
                                        w2_all[:, bass.ds(expert(t, words[1]), 1), q, :].rearrange("p a d -> p (a d)"), start=q == 0, stop=q == 1)
                    ins.then_inc(S.out_done, 1)
            words = [0, 0]
            pe.wait_ge(S.table_ready, 2)
            transpose_rows(Tile(0, 0, XR))
            transpose_rows(Tile(0, 1, XR))
            run_steps(pe, step, NT + 1, EXPERT_LOOP)

        @block.scalar
        def _(act):
            def copy(o, i, scale=1.0):
                return act.activation(o, i, ACT.Copy, scale=scale)

            act.wait_ge(S.consts_made, 4)
            act.activation(warm[:], iota8[:, 0:1], ACT.Sqrt, bias=EPS).then_inc(S.table_warm, 1)
            act.wait_ge(S.set_done, 1)
            copy(wT[:, :, :], tok_ps[:, :].rearrange("p (q d) -> p q d", q=2 * NH)).then_inc(S.set_copied, 1)
            def copy_xT(t):
                wait_for(act, S.xT_done, t.index + 1)
                if t.static and t.index == TILES:
                    copy(xT[:, (t.slot - 1) % RING, :, P:P + B], xT_ps[:, :, 0:B]).then_inc(S.xT_copied, 1)
                    return
                ins = copy(xT[:, t.slot, :, 0:P], xT_ps)
                if not t.static or t.index > 0:
                    ins = copy(xT[:, (t.slot - 1) % RING, :, P:P + B], xT_ps[:, :, 0:B])
                ins.then_inc(S.xT_copied, 1)

            def step(rnd, s):
                if t := tile(rnd, s, 5):
                    wait_for(act, S.xsT_done, t.index + 1)
                    copy(xsT[:, :, :], XSP, scale=E2).then_inc(S.xsT_copied, 1)
                if t := tile(rnd, s, 2):
                    wait_for(act, S.mom1_ready, t.index + 1)
                    act.activation(std1[:], mom1[:, 1:2], ACT.Sqrt, bias=EPS).then_inc(S.std1_ready, 1)
                if t := tile(rnd, s, 6):
                    wait_for(act, S.mom2_ready, t.index + 1)
                    act.activation(std2[:], mom2[:, 1:2], ACT.Sqrt, bias=EPS).then_inc(S.std2_ready, 1)
                if t := tile(rnd, s, 3):
                    wait_for(act, S.even_done, t.index + 1)
                    copy(XT[:, t.slot, :, 0:P // 2], V[:, :, 0:P // 2]).then_inc(S.even_copied, 1)
                if t := tile(rnd, s, 7):
                    wait_for(act, S.nT_done, t.index + 1)
                    copy(nT[:], n_ps[:, 0:P])
                    copy(nT_all[:, bass.ds(t.index, 1), :].rearrange("p a d -> p (a d)"), n_ps[:, 0:P]).then_inc(S.nT_copied, 1)
                if t := tile(rnd, s, 3):
                    wait_for(act, S.odd_done, t.index + 1)
                    copy(XT[:, t.slot, :, P // 2:P], V[:, :, P // 2:P]).then_inc(S.odd_copied, 1)
                if t := tile(rnd, s, 2):
                    wait_for(act, S.uT_done, t.index + 1)
                    copy(uT[:, t.slot, B:B + P], uT_ps[:, 0:P])
                    copy(uT[:, (t.slot + 1) % RING, 0:B], uT_ps[:, P - B:P]).then_inc(S.uT_copied, 1)
                if t := tile(rnd, s, -1, TILES + 1):
                    copy_xT(t)
                if t := tile(rnd, s, 6):
                    wait_for(act, S.shift2_ready, t.index + 1)
                    if not t.static or t.index >= RING:
                        wait_for(act, scattered[t.slot], t.turn * 32)
                    h2 = h2_all[:, bass.ds(t.index, 1), :].rearrange("p a d -> p (a d)")
                    act.activation(send[:, t.slot, 0, 0:D], h2, ACT.Identity, bias=shift2[:], scale=inv2[:]).then_inc(S.xn_ready, 1)

            copy_xT(Tile(0, 0))
            step(0, 0)
            step(0, 1)
            act.wait_ge(S.set_done, 2)
            copy(adT[:], y_ps[:, 0:P])
            copy(gateT[:], y_ps[:, 3 * P:3 * P + E]).then_inc(S.set_copied, 1)
            copy(bT[:, :, :], y_ps[:, P:3 * P].rearrange("p (q d) -> p q d", q=NPAIR)).then_inc(S.set_copied, 1)
            act.wait_ge(S.set_done, 3)
            copy(a2d[:], y_ps[:, 0:P])
            copy(ba[:, :, :], y_ps[:, P:3 * P].rearrange("p (q d) -> p q d", q=NPAIR)).then_inc(S.set_copied, 1)
            run_steps(act, step, TILES + 6, start=2)

            act.wait_ge(S.topv_ready, TILES)
            act.activation(sig[:, :, :], topv_all[:, :, :], ACT.Sigmoid).then_inc(S.sig_ready, 1)

            def step(rnd, s):
                if t := tile(rnd, s, 0):
                    wait_for(act, S.sup_done, t.index + 1)
                    if not t.static or t.index >= 2:
                        wait_for(act, S.shid_ready, t.index - 1)
                    act.activation(act_h[:, t.slot % 2, :], up_ps[t.slot % 2][:, 0:2 * P], ACT.Silu).then_inc(S.sact_ready, 1)
            run_steps(act, step, TILES - 1, SHARED_LOOP)

            def copy_rows(t):
                wait_for(act, S.xgT_done, t.index + 1)
                copy(xgT[:, t.slot, :], rows_ps[t.slot % 2][:, 0:P]).then_inc(S.xgT_copied, 1)

            def step(rnd, s):
                if t := tile(rnd, s, 0, NT, XR):
                    wait_for(act, S.up_done, t.index + 1)
                    wait_for(act, S.hid_ready, t.index - 1)
                    act.activation(act_h[:, t.slot % 2, :], up_ps[t.slot % 2][:, 0:2 * P], ACT.Silu).then_inc(S.act_ready, 1)
                if t := tile(rnd, s, -2, NT, XR):
                    copy_rows(t)
                if t := tile(rnd, s, 1, NT, XR):
                    wait_for(act, S.hidT_done, t.index + 1)
                    wait_for(act, S.out_done, t.index - 1)
                    copy(hidT[:, t.slot % 2, :, :].rearrange("p q n -> p (q n)"), hidT_ps[t.slot % 2][:, 0:2 * P]).then_inc(S.hidT_copied, 1)
                if t := tile(rnd, s, 2, NT, XR):
                    wait_for(act, S.out_done, t.index + 1)
                    if not t.static or t.index >= XR:
                        wait_for(act, sent_back[t.slot], t.turn * 16)
                    copy(yo[:, t.slot, :], down_ps[t.slot % 2][:, 0:D]).then_inc(S.yo_ready, 1)
            copy_rows(Tile(0, 0, XR))
            copy_rows(Tile(0, 1, XR))
            run_steps(act, step, NT + 1, EXPERT_LOOP[:3] + (2,))

            store(act, DVE_STORES, S.fin_ready, 0, S.out_stored)

        @block.vector
        def _(dve):
            dve.wait_ge(S.consts_made, CONSTS)
            dve.wait_ge(S.tok_b_loaded, 16)

            def step(rnd, s):
                ln1, ln2, srt, cho, mx = (tile(rnd, s, lag) for lag in (2, 6, 8, 7, 4))
                if t := ln1:
                    h1 = h2_all[:, bass.ds(t.index, 1), :].rearrange("p a d -> p (a d)")
                    wait_for(dve, S.tok_done, t.index + 1)
                    dve.tensor_tensor(h1, tok_ps[:, 0:D], tok_b_bc[:], ALU.add).then_inc(S.h_ready, 1)
                if t := srt:
                    wait_alone(dve, S.topi_ready, t.index + 1)
                    pick = pick_all[:, bass.ds(t.index, 1), :, :].rearrange("p a j e -> p (a j) e")
                    dve.tensor_tensor(pick, iota8[:].unsqueeze(1).to_broadcast([P, 2, E]),
                                      top_i[:, 0:2].unsqueeze(2).to_broadcast([P, 2, E]), ALU.is_equal).then_inc(S.pick_ready, 1)
                if t := ln2:
                    h2 = h2_all[:, bass.ds(t.index, 1), :].rearrange("p a d -> p (a d)")
                    wait_for(dve, S.y_done, t.index + 1)
                    dve.tensor_tensor(h2, y_ps[:, 0:D], h2, ALU.add).then_inc(S.h2_ready, 1)
                if t := srt:
                    wait_for(dve, S.pick_ready, t.index + 1)
                    dve.tensor_tensor(oh[:], pick[:, 0, :], pick[:, 1, :], ALU.add).then_inc(S.oh_ready, 1)
                if t := ln1:
                    wait_alone(dve, S.h_ready, t.index + 1)
                    dve.bn_stats(stats1[:], h1).then_inc(S.stats1_ready, 1)
                if t := ln2:
                    wait_alone(dve, S.h2_ready, t.index + 1)
                    dve.bn_stats(stats2[:], h2).then_inc(S.stats2_ready, 1)
                if t := ln1:
                    wait_alone(dve, S.stats1_ready, t.index + 1)
                    dve.bn_aggr(mom1[:], stats1[:]).then_inc(S.mom1_ready, 1)
                if t := ln2:
                    wait_alone(dve, S.stats2_ready, t.index + 1)
                    dve.bn_aggr(mom2[:], stats2[:]).then_inc(S.mom2_ready, 1)
                if t := mx:
                    wait_for(dve, S.xtok_done, t.index + 1)
                    xh = xtok_ps[:, 0:NPAIR * P].rearrange("p (h d) -> p h d", h=HEADS)
                    dve.tensor_reduce(rowmax[:], xh, AX_X, ALU.max, apply_absolute_value=True).then_inc(S.rowmax_ready, 1)
                if t := ln1:
                    wait_for(dve, S.std1_ready, t.index + 1)
                    dve.reciprocal(inv1[:], std1[:]).then_inc(S.inv1_ready, 1)
                if t := ln2:
                    wait_for(dve, S.std2_ready, t.index + 1)
                    dve.reciprocal(inv2[:], std2[:]).then_inc(S.inv2_ready, 1)
                if t := mx:
                    wait_for(dve, S.rowmax_ready, t.index + 1)
                    dve.reciprocal(rowinv[:], rowmax[:]).then_inc(S.rowinv_ready, 1)
                if t := ln1:
                    wait_for(dve, S.inv1_ready, t.index + 1)
                    dve.tensor_scalar(u[:, t.slot, :], h1, mom1[:, 0:1], inv1[:, 0:1], ALU.subtract, ALU.mult).then_inc(S.u_ready, 1)
                if t := ln2:
                    wait_for(dve, S.inv2_ready, t.index + 1)
                    dve.tensor_scalar(shift2[:], mom2[:, 0:1], inv2[:, 0:1], -1.0, ALU.mult, ALU.mult).then_inc(S.shift2_ready, 1)
                if t := mx:
                    wait_for(dve, S.rowinv_ready, t.index + 1)
                    dve.tensor_tensor(xs[:].rearrange("p (h d) -> p h d", h=HEADS), xh,
                                      rowinv[:].unsqueeze(2).to_broadcast([P, HEADS, DH]), ALU.mult).then_inc(S.xs_ready, 1)
                if t := srt:
                    wait_for(dve, S.rank_done, t.index + 1)
                    wait_for(dve, S.rank_read, t.index)
                    dve.tensor_tensor(ranked[:], uT_ps[:, P:P + E], base[:], ALU.add).then_inc(S.ranked_ready, 1)
                    dve.tensor_tensor(base[:], base[:], uT_ps[:, P + E:P + 2 * E], ALU.add).then_inc(S.rank_read, 1)
                if t := cho:
                    wait_for(dve, S.gate_done, t.index + 1)
                    dve.tensor_tensor(biased[:], n_ps[:, 2 * P:2 * P + E], gate_b_bc[:], ALU.add).then_inc(S.biased_ready, 1)
                    if not t.static or t.index >= RING - 1:
                        wait_alone(dve, S.topv_ready, t.index - RING + 2)
                    dve.max(top_s[:, t.slot, :], n_ps[:, 2 * P:2 * P + E]).then_inc(S.scores_read, 1)
                if t := srt:
                    wait_for(dve, S.ranked_ready, t.index + 1)
                    pick = pick_all[:, bass.ds(t.index, 1), :, :].rearrange("p a j e -> p (a j) e")
                    dve.tensor_tensor(junk[:, :, :], pick, ranked[:].unsqueeze(1).to_broadcast([P, 2, E]), ALU.mult).then_inc(S.pickrank_ready, 1)
                if t := cho:
                    wait_alone(dve, S.biased_ready, t.index + 1)
                    dve.max(top_b[:], biased[:]).then_inc(S.top_ready, 1)
                if t := srt:
                    wait_for(dve, S.pickrank_ready, t.index + 1)
                    slots = slot_all[:, bass.ds(t.index, 1), :].rearrange("p a j -> p (a j)")
                    dve.tensor_reduce(slots, junk[:, :, :], AX_X, ALU.add).then_inc(S.slots_ready, 1)
                if t := cho:
                    wait_alone(dve, S.top_ready, t.index + 1)
                    dve.max_index(top_i[:], top_b[:], biased[:]).then_inc(S.topi_ready, 1)

            step(0, 2)
            dve.wait_ge(S.small_loaded, 16 * 5)
            for q in range(NPAIR):
                ins = dve.tensor_copy(XT[:, RING - 1, q, P - B:P], x0[:, q:q + 1].to_broadcast([P, B]))
            ins.then_inc(S.set_vec, 1)
            dve.wait_ge(S.late_loaded, 16 * 3)
            run_steps(dve, step, TILES + 7, start=3)

            dve.wait_ge(S.rank_read, TILES)
            dve.tensor_tensor(pad_i[:], base[:], pad_at[:], ALU.add).then_inc(S.pads_ready, 1)

            made = 0

            def link(ins):
                nonlocal made
                made += 1
                ins.then_inc(S.tables_made, 1)
                dve.wait_ge(S.tables_made, made)

            def over(ap, n):
                return ap.unsqueeze(1).to_broadcast([1, n, E])

            link(dve.tensor_tensor(cnt_f[:], base[0:1, :], region_at[0:1, :], ALU.subtract))
            link(dve.tensor_scalar(cnt_i[:], cnt_f[:], float(P - 1), None, ALU.add))
            link(dve.tensor_scalar(cnt_s[:], cnt_i[:], P.bit_length() - 1, None, ALU.arith_shift_right))
            link(dve.tensor_copy(ntile[:], cnt_s[:]))
            link(dve.tensor_tensor(ends_m[:, :, :], upto[:, :, :], over(ntile[:], E), ALU.mult))
            link(dve.tensor_reduce(ends[:], ends_m[:, :, :], AX_X, ALU.add))
            link(dve.tensor_tensor(past[:, :, :], tile_no[:].unsqueeze(2).to_broadcast([1, COLS, E]), over(ends[:], COLS), ALU.is_ge))
            link(dve.tensor_reduce(t_exp[:], past[:, :, :], AX_X, ALU.add))
            link(dve.tensor_tensor(past_n[:, :, :], past[:, :, :], over(ntile[:], COLS), ALU.mult))
            link(dve.tensor_reduce(t_first[:], past_n[:, :, :], AX_X, ALU.add))
            link(dve.scalar_tensor_tensor(out=t_row[:], in0=tile_no[:], scalar=1.0, in1=t_first[:], op0=ALU.add, op1=ALU.subtract))
            link(dve.tensor_scalar(t_valid[:], t_exp[:], float(E), None, ALU.is_lt))
            link(dve.tensor_tensor(t_row[:], t_row[:], t_valid[:], ALU.mult))
            link(dve.scalar_tensor_tensor(out=t_row[:], in0=t_exp[:], scalar=float(RTILES), in1=t_row[:], op0=ALU.mult, op1=ALU.add))
            link(dve.tensor_scalar(t_row[:], t_row[:], -1.0, None, ALU.add))
            link(dve.tensor_scalar(t_exp[:], t_exp[:], float(E - 1), None, ALU.min))

            def pack(o, i, radix, first=0):
                pairs = i[:, first:first + 2 * o.shape[1]].rearrange("a (n two) -> a n two", two=2)
                return dve.scalar_tensor_tensor(out=o[:], in0=pairs[:, :, 1], scalar=float(radix), in1=pairs[:, :, 0], op0=ALU.mult, op1=ALU.add)

            pack(row_words, t_row, ROW_RADIX, first=2).then_inc(S.table_ready, 1)
            link(pack(e_pair, t_exp, E))
            link(pack(e_four, e_pair, E ** 2))
            pack(expert_words, e_four, E ** 4).then_inc(S.table_ready, 1)

            dve.wait_ge(S.sig_ready, 1)
            link(dve.tensor_tensor(sig_sum[:], sig[:, :, 0], sig[:, :, 1], ALU.add))
            link(dve.reciprocal(sig_inv[:], sig_sum[:]))
            dve.tensor_tensor(prob[:, :, :], sig[:, :, :], sig_inv[:].unsqueeze(2).to_broadcast([P, TILES, 2]), ALU.mult).then_inc(S.prob_ready, 1)

            def gate_hidden(t, done):
                dve.tensor_tensor(hid[:, t.slot % 2, :, :].rearrange("p q n -> p (q n)"), act_h[:, t.slot % 2, :],
                                  up_ps[t.slot % 2][:, 2 * P:4 * P], ALU.mult).then_inc(done, 1)

            def step(rnd, s):
                if t := tile(rnd, s, 0):
                    wait_for(dve, S.sact_ready, t.index + 1)
                    wait_for(dve, S.sout_done, t.index - 1)
                    gate_hidden(t, S.shid_ready)
                if t := tile(rnd, s, 1):
                    wait_for(dve, S.sout_done, t.index + 1)
                    h2 = h2_all[:, bass.ds(t.index, 1), :].rearrange("p a d -> p (a d)")
                    dve.tensor_tensor(h2, down_ps[t.slot % 2][:, 0:D], h2, ALU.add).then_inc(S.sadded, 1)
            run_steps(dve, step, TILES, SHARED_LOOP)

            def step(rnd, s):
                t = Tile(rnd, s, XR)
                wait_for(dve, S.act_ready, t.index + 1)
                wait_for(dve, S.hidT_done, t.index - 1)
                gate_hidden(t, S.hid_ready)
            run_steps(dve, step, NT - 1, EXPERT_LOOP)

            dve.wait_ge(S.prob_ready, 1)
            dve.wait_ge(S.sadded, TILES)

            for k0, k1 in DVE_LOADS:
                dve.wait_ge(yin_loaded[k0, k1], 16)
                for k in range(k0, k1):
                    dve.scalar_tensor_tensor(out=h2_all[:, k, :], in0=yin[:, k, 0, :], scalar=prob[:, k, 0:1], in1=h2_all[:, k, :],
                                             op0=ALU.mult, op1=ALU.add).then_inc(S.mid_ready, 1)
                for k in range(k0, k1):
                    dve.wait_ge(S.mid_ready, k + 1)
                    dve.scalar_tensor_tensor(out=h2_all[:, k, :], in0=yin[:, k, 1, :], scalar=prob[:, k, 1:2], in1=h2_all[:, k, :],
                                             op0=ALU.mult, op1=ALU.add).then_inc(S.fin_ready, 1)


_INS = ["x", "L0_tok_W", "L0_tok_b", "L0_attn_init_states", "L0_attn_A", "L0_attn_B", "L0_attn_C", "L0_attn_D",
        "L0_ffn_gate_w", "L0_ffn_biases", "L0_ffn_w1", "L0_ffn_w3", "L0_ffn_w2", "L0_ffn_sw1", "L0_ffn_sw3", "L0_ffn_sw2"]
_OUT = ((32, 92, 128), "float32")


def kernel(**inputs):
    import numpy as _np
    import concourse.bacc as _bacc
    from concourse import mybir as _mybir
    from concourse.bass_utils import run_bass_kernel_spmd as _run

    nc = _bacc.Bacc("TRN2", target_bir_lowering=False, num_devices=1)
    arrays, args = {}, []
    for name in _INS:
        a = _np.ascontiguousarray(inputs[name])
        arrays[f"in_{name}_dram"] = a
        args.append(nc.dram_tensor(f"in_{name}_dram", a.shape, _mybir.dt.from_np(a.dtype), kind="ExternalInput").ap())
    shape, dtype = _OUT
    args.append(nc.dram_tensor("out_dram", shape, _mybir.dt.from_np(_np.dtype(dtype)), kind="ExternalOutput").ap())
    audio_tower_kernel(nc, *args)
    r = _run(nc, [arrays], core_ids=[0])
    return r.results[0]["out_dram"]
```
